# Optimizing a Trainium2 kernel written in Bass

```python
import numpy as np
import jax
import jax.numpy as jnp

def _softmax(x, axis=-1):
    return jax.nn.softmax(x, axis=axis)

def _gelu(x):
    return jax.nn.gelu(x, approximate=True)

def _silu(x):
    return jax.nn.silu(x)

def _sigmoid(x):
    return jax.nn.sigmoid(x)

def _layernorm(x, axis=-1, eps=1e-05):
    m = jnp.mean(x, axis=axis, keepdims=True)
    v = jnp.var(x, axis=axis, keepdims=True)
    return (x - m) / jnp.sqrt(v + eps)

def _scatter_add(tgt, idx, src, axis=0):
    return tgt.at[idx].add(src)

def _segment_sum(src, seg, n):
    return jax.ops.segment_sum(src, seg, n)
kernel_name = 'mk_seq_postln_d1_jaxref_r4_38ffe3'

def setup_inputs(seed: int=0):
    np.random.seed(seed)
    _w = jnp.asarray

    def _L0_attn_setup():
        import math
        import jax, jax.numpy as jnp
        import numpy as np
        B, T, C = (2, 512, 256)
        H, N1, N2, N3 = (16, 6, 4, 6)
        HD = C // H

        def _rotary(T_, hd, dtype):
            inv_freq = 1.0 / 10000.0 ** (jnp.arange(0, hd, 2, dtype=jnp.float32) / hd)
            freqs = jnp.outer(jnp.arange(T_, dtype=jnp.float32), inv_freq)
            return (jnp.cos(freqs)[None, :, None, :].astype(dtype), jnp.sin(freqs)[None, :, None, :].astype(dtype))

        def _apply_rot(x, cos, sin):
            x1, x2 = (x[..., :x.shape[-1] // 2], x[..., x.shape[-1] // 2:])
            return jnp.concatenate([x1 * cos + x2 * sin, -x1 * sin + x2 * cos], axis=-1).astype(x.dtype)

        def _causal_bias(L, S, dtype):
            mask = jnp.triu(jnp.ones((L, S), bool), k=1)
            return jnp.where(mask, jnp.asarray(-jnp.inf, dtype), jnp.asarray(0.0, dtype))

        def _sdpa(q, k, v, scale):
            scores = jnp.einsum('bhtd,bhsd->bhts', q, k) * scale + _causal_bias(q.shape[-2], k.shape[-2], q.dtype)
            return jnp.einsum('bhts,bhsd->bhtd', jax.nn.softmax(scores, axis=-1), v)

        def _hyp_attn(q, k, v, curv):
            eps = 1e-06
            tq = jnp.sqrt(1.0 / curv + jnp.sum(q * q, axis=-1, keepdims=True))
            tk = jnp.sqrt(1.0 / curv + jnp.sum(k * k, axis=-1, keepdims=True))
            inner = jnp.einsum('bhtd,bhsd->bhts', q, k) - tq * jnp.swapaxes(tk, -1, -2)
            arg = jnp.maximum(-curv * inner, 1.0 + 1e-07)
            dis = jnp.sqrt(1.0 / curv) * jnp.arccosh(arg)
            scores = 1.0 / (eps + dis) + _causal_bias(q.shape[-2], k.shape[-2], q.dtype)
            return jnp.einsum('bhts,bhsd->bhtd', jax.nn.softmax(scores, axis=-1), v)
        key = jax.random.key(seed)
        k1, k2, k3 = jax.random.split(key, 3)
        return {'x': jax.random.normal(k1, (B, T, C), jnp.float32), 'qkv_w': jax.random.normal(k2, (3 * C, C), jnp.float32) * C ** (-0.5), 'proj_w': jax.random.normal(k3, (C, C), jnp.float32) * C ** (-0.5), 'proj_b': jnp.zeros((C,), jnp.float32), 'curvature': jnp.ones((1, N2, 1, 1), jnp.float32)}
    _L0_attn_in = _L0_attn_setup()

    def _L0_ffn_setup():
        import jax, jax.numpy as jnp
        import numpy as np
        SL, BS, HS, FF, E, TOPK = (512, 2, 256, 1024, 8, 2)
        key = jax.random.key(seed)
        ks = jax.random.split(key, 6)
        T = SL * BS
        x = jax.random.normal(ks[0], (SL, BS, HS), jnp.float32)
        scores = jax.random.uniform(ks[1], (T, E), jnp.float32)
        expert_weights = jax.random.uniform(ks[2], (T, TOPK), jnp.float32)
        expert_indices = jax.random.randint(ks[3], (T, TOPK), 0, E, jnp.int32)
        w1 = jax.random.normal(ks[4], (E, HS, FF), jnp.float32) * (1.0 / np.sqrt(HS))
        w2 = jax.random.normal(ks[5], (E, FF, HS), jnp.float32) * (1.0 / np.sqrt(FF))
        bias = jnp.zeros((HS,), jnp.float32)
        return dict(x=x, scores=scores, expert_weights=expert_weights, expert_indices=expert_indices, w1=w1, w2=w2, bias=bias)
    _L0_ffn_in = _L0_ffn_setup()
    _d = {'L0_attn_x': _L0_attn_in['x'], 'L0_attn_qkv_w': _L0_attn_in['qkv_w'], 'L0_attn_proj_w': _L0_attn_in['proj_w'], 'L0_attn_proj_b': _L0_attn_in['proj_b'], 'L0_attn_curvature': _L0_attn_in['curvature'], 'L0_ffn_scores': _L0_ffn_in['scores'], 'L0_ffn_expert_weights': _L0_ffn_in['expert_weights'], 'L0_ffn_expert_indices': _L0_ffn_in['expert_indices'], 'L0_ffn_w1': _L0_ffn_in['w1'], 'L0_ffn_w2': _L0_ffn_in['w2'], 'L0_ffn_bias': _L0_ffn_in['bias']}
    _x0 = _d['L0_attn_x']
    _d['L0_attn_x'] = jax.random.normal(jax.random.fold_in(jax.random.key(seed), 1), (8, 1024, 256), dtype=_x0.dtype)
    del _x0
    return _d

def reference(L0_attn_x, L0_attn_qkv_w, L0_attn_proj_w, L0_attn_proj_b, L0_attn_curvature, L0_ffn_scores, L0_ffn_expert_weights, L0_ffn_expert_indices, L0_ffn_w1, L0_ffn_w2, L0_ffn_bias):

    def _L0_attn_ref(x, qkv_w, proj_w, proj_b, curvature):
        import math
        import jax, jax.numpy as jnp
        import numpy as np
        B, T, C = (2, 512, 256)
        H, N1, N2, N3 = (16, 6, 4, 6)
        HD = C // H

        def _rotary(T_, hd, dtype):
            inv_freq = 1.0 / 10000.0 ** (jnp.arange(0, hd, 2, dtype=jnp.float32) / hd)
            freqs = jnp.outer(jnp.arange(T_, dtype=jnp.float32), inv_freq)
            return (jnp.cos(freqs)[None, :, None, :].astype(dtype), jnp.sin(freqs)[None, :, None, :].astype(dtype))

        def _apply_rot(x, cos, sin):
            x1, x2 = (x[..., :x.shape[-1] // 2], x[..., x.shape[-1] // 2:])
            return jnp.concatenate([x1 * cos + x2 * sin, -x1 * sin + x2 * cos], axis=-1).astype(x.dtype)

        def _causal_bias(L, S, dtype):
            mask = jnp.triu(jnp.ones((L, S), bool), k=1)
            return jnp.where(mask, jnp.asarray(-jnp.inf, dtype), jnp.asarray(0.0, dtype))

        def _sdpa(q, k, v, scale):
            scores = jnp.einsum('bhtd,bhsd->bhts', q, k) * scale + _causal_bias(q.shape[-2], k.shape[-2], q.dtype)
            return jnp.einsum('bhts,bhsd->bhtd', jax.nn.softmax(scores, axis=-1), v)

        def _hyp_attn(q, k, v, curv):
            eps = 1e-06
            tq = jnp.sqrt(1.0 / curv + jnp.sum(q * q, axis=-1, keepdims=True))
            tk = jnp.sqrt(1.0 / curv + jnp.sum(k * k, axis=-1, keepdims=True))
            inner = jnp.einsum('bhtd,bhsd->bhts', q, k) - tq * jnp.swapaxes(tk, -1, -2)
            arg = jnp.maximum(-curv * inner, 1.0 + 1e-07)
            dis = jnp.sqrt(1.0 / curv) * jnp.arccosh(arg)
            scores = 1.0 / (eps + dis) + _causal_bias(q.shape[-2], k.shape[-2], q.dtype)
            return jnp.einsum('bhts,bhsd->bhtd', jax.nn.softmax(scores, axis=-1), v)
        Bx, Tx, Cx = x.shape
        qkv = x @ qkv_w.T
        q, k, v = jnp.split(qkv, 3, axis=-1)
        q = q.reshape(Bx, Tx, H, HD)
        k = k.reshape(Bx, Tx, H, HD)
        v = v.reshape(Bx, Tx, H, HD)
        cos, sin = _rotary(Tx, HD, x.dtype)
        q = _apply_rot(q, cos, sin)
        k = _apply_rot(k, cos, sin)
        q, k, v = (jnp.swapaxes(t, 1, 2) for t in (q, k, v))
        outs = []
        outs.append(_sdpa(q[:, :N1], k[:, :N1], v[:, :N1], 1.0 / math.sqrt(HD)))
        outs.append(_hyp_attn(q[:, N1:N1 + N2], k[:, N1:N1 + N2], v[:, N1:N1 + N2], curvature))
        qn = q[:, N1 + N2:] / jnp.maximum(jnp.linalg.norm(q[:, N1 + N2:], axis=-1, keepdims=True), 1e-12)
        kn = k[:, N1 + N2:] / jnp.maximum(jnp.linalg.norm(k[:, N1 + N2:], axis=-1, keepdims=True), 1e-12)
        outs.append(_sdpa(qn, kn, v[:, N1 + N2:], math.sqrt(HD)))
        y = jnp.concatenate(outs, axis=1)
        y = jnp.swapaxes(y, 1, 2).reshape(Bx, Tx, Cx)
        return y @ proj_w.T + proj_b

    def _L0_ffn_ref(x, scores, expert_weights, expert_indices, w1, w2, bias):
        import jax, jax.numpy as jnp
        import numpy as np
        SL, BS, HS, FF, E, TOPK = (512, 2, 256, 1024, 8, 2)
        sl, bs, hs = x.shape
        n_exp = w1.shape[0]
        top_k = expert_indices.shape[-1]
        xf = x.reshape(-1, hs)
        flat_idx = expert_indices.reshape(-1)
        flat_w = expert_weights.reshape(-1)
        order = jnp.argsort(flat_idx)
        tok = order // top_k
        tokens_per_expert = jnp.bincount(flat_idx, length=n_exp).astype(jnp.int32)
        xs = xf[tok]
        h = jax.nn.gelu(jax.lax.ragged_dot(xs, w1, tokens_per_expert), approximate=False)
        ys = jax.lax.ragged_dot(h, w2, tokens_per_expert)
        ys = ys * flat_w[order][:, None]
        out = jnp.zeros_like(xf).at[tok].add(ys)
        return out.reshape(sl, bs, hs) + bias
    x = L0_attn_x
    x = _layernorm(x + _L0_attn_ref(x, L0_attn_qkv_w, L0_attn_proj_w, L0_attn_proj_b, L0_attn_curvature), axis=-1)
    x = _layernorm(x + _L0_ffn_ref(x, L0_ffn_scores, L0_ffn_expert_weights, L0_ffn_expert_indices, L0_ffn_w1, L0_ffn_w2, L0_ffn_bias), axis=-1)
    return x

_drawn_inputs = setup_inputs


def setup_inputs(seed=0):
    import zlib

    import numpy as np

    out = dict(_drawn_inputs(seed))
    spreads = {'L0_attn_proj_b': (0.0, 0.1), 'L0_attn_curvature': (1.0, 0.2), 'L0_ffn_bias': (0.0, 0.1)}
    factors = {}
    for name, (base, spread) in spreads.items():
        noise = np.random.default_rng([zlib.crc32(name.encode()), seed]).standard_normal(out[name].shape)
        drawn = base * np.exp(spread * noise) if base else spread * noise
        out[name] = jnp.asarray(drawn.astype(out[name].dtype))
    for name, factor in factors.items():
        out[name] = (out[name] * factor).astype(out[name].dtype)
    return out
```

```python
from contextlib import ExitStack

import numpy as np
import concourse.bass as bass
from concourse import mybir

F32 = mybir.dt.float32
BF16 = mybir.dt.bfloat16
I32 = mybir.dt.int32
ALU = mybir.AluOpType
ACT = mybir.ActivationFunctionType
AX = mybir.AxisListType

P = 128
B, T, C = 8, 1024, 256
H, HD = 16, 16
N_DOT, N_HYP = 6, 4
N_COS = H - N_DOT - N_HYP
HYP0, COS0 = N_DOT, N_DOT + N_HYP
NT = T // P
CK = C // P
HB = 512
GW = P // HD
QPART = (0, 0, 1, 0, 2, 1)
KPART = (0, 1, 0, 2, 0, 1)
NPAIR = len(QPART)
KR = NPAIR * HD
NE, TOPK, FF = 8, 2, 1024
N_TOK = 1024
TINY = 1e-24
HYP_GROUP = tuple(range(HYP0, COS0))
GROUPS = ((12, 13, 14, 15), (0, 1, 2, 3), (10, 11, 4, 5), HYP_GROUP)
PACKED = tuple(h for g in GROUPS for h in g)
VW = 32


class Event:

    def __init__(self, ctx, nc, name, per=1, step=1, carried=False):
        self.sem = ctx.enter_context(nc.semaphore(name))
        self.per, self.step, self.carried = per, step, carried

    def start(self, engine):
        assert self.carried
        engine.sem_inc(self.sem, self.per * self.step)

    def at(self, turn, k=0):
        return turn * (self.per * self.step) + (k + 1 + self.per * self.carried) * self.step

    def before(self, turn, k=0):
        assert self.carried
        return turn * (self.per * self.step) + (k + 1) * self.step


def hold(engine, semaphore, value, passed):
    engine.wait_ge(semaphore, value)
    engine.sem_inc(passed, 1)


def project(nc, io, qk_parts, t_parts, v_rows, rk_cols):
    with ExitStack() as ctx:
        def sb(name, shape, dt=F32):
            return ctx.enter_context(nc.sbuf_tensor(name, shape, dt))

        def ev(name, per=1, step=1, carried=False):
            return Event(ctx, nc, name, per, step, carried)

        G = 4
        W_COL = (1, 0, 2, 3)
        SPLIT = (1, 0, 2, 3)
        ident = sb("p_ident", [P, P])
        w = sb("p_w", [P, CK, 5 * C])
        tabs = sb("p_tabs", [P, 2, T])
        ktabs = sb("p_ktabs", [P, 2, 2, T])
        kcurv = sb("p_kcurv", [P, 2, 2])
        kfac = sb("p_kfac", [P, 2])
        rcurv = sb("p_rcurv", [16, 3])
        radd = sb("p_radd", [16, 3])
        rowind = sb("p_rowind", [P, G, 16])
        blk = sb("p_blk", [P, P])
        nhyp = sb("p_nhyp", [P, 1])
        xin = sb("p_xin", [P, NT, C])
        xT = sb("p_xT", [P, CK, T])
        prod = sb("p_prod", [P, 2, T])
        rot = sb("p_rot", [P, G, T])
        sq = sb("p_sq", [P, G, T])
        fac = sb("p_fac", [P, T])
        parts = sb("p_parts", [P, 2, 3, T], BF16)
        rest = sb("p_rest", [P, T])
        vt = sb("p_vt", [P, 4, NT, 4, VW])
        ra = sb("p_ra", [16, T])
        rr = sb("p_rr", [16, T])
        rt = sb("p_rt", [16, T])
        tp = sb("p_tp", [16, 3, T], BF16)
        rk = sb("p_rk", [P, NT, N_COS])
        slot = [ctx.enter_context(nc.psum_tensor(f"p_ps{i}", [P, 2 * HB], F32)) for i in range(4)]

        consts = ctx.enter_context(nc.semaphore("p_consts"))
        NCONST = 9
        setup_dve = ctx.enter_context(nc.semaphore("p_setup_dve"))
        pool_passed = ctx.enter_context(nc.semaphore("p_pool_passed"))
        pe_passed = ctx.enter_context(nc.semaphore("p_pe_passed"))
        x_here = ev("p_x_here", 1, 16)
        x_turned = ev("p_x_turned", 2, carried=True)
        xt_ready = ev("p_xt_ready", 2)
        qk_ready = ev("p_qk_ready", 2 * G)
        v_ready = ev("p_v_ready", 2, carried=True)
        mul_done = ev("p_mul_done", 2 * G)
        rot_ready = ev("p_rot_ready", G, carried=True)
        sq_ready = ev("p_sq_ready", G)
        norm_ready, fac_max, fac_ln, fac_exp = ev("p_norm"), ev("p_fac_max"), ev("p_fac_ln"), ev("p_fac_exp")
        q_scaled = ev("p_q_scaled")
        hi_ready, rest_ready, mid_ready = ev("p_hi", G), ev("p_rest_r", G), ev("p_mid", G)
        lo_ready = ev("p_lo", G, carried=True)
        parts_sent = [ev(f"p_parts_sent{k}", 2, 16, carried=True) for k in range(2)]
        v_copied = ev("p_v_copied", 2)
        v_sent = ev("p_v_sent", 1, 16, carried=True)
        rows_ready = ev("p_rows", carried=True)
        ra_ready, r_ln, r_exp = ev("p_ra_r"), ev("p_r_ln"), ev("p_r_exp")
        r_step = ev("p_r_step", 9, carried=True)
        cols_ready, rk_ready = ev("p_cols", carried=True), ev("p_rk_r", carried=True)
        tp_sent, rk_sent = ev("p_tp_sent", 1, 16, carried=True), ev("p_rk_sent", 1, 16, carried=True)
        block = ctx.enter_context(nc.Block())

        @block.sync
        def _(sp):
            for dst, name in ((ident, "ident"), (w, "w_qkv"), (tabs, "tabs"), (kcurv, "kcurv"), (rcurv, "rcurv"),
                              (rowind, "rowind"), (blk, "blk"), (nhyp, "nhyp")):
                sp.dma_start(dst[:], io[name]).then_inc(consts, 16)
            sp.dma_start(vt[:], io["v_pad"]).then_inc(consts, 16)
            for k in range(2):
                parts_sent[k].start(sp)
            v_sent.start(sp)
            tp_sent.start(sp)
            rk_sent.start(sp)
            with sp.Fori(0, B) as b:
                sp.wait_ge(x_turned.sem, x_turned.before(b, 1))
                sp.dma_start(xin[:], io["x"][bass.ds(b, 1)].rearrange("o (n p) c -> p (o n) c", p=P)) \
                    .then_inc(x_here.sem, 16)
                for k, g in enumerate(SPLIT):
                    sp.wait_ge(lo_ready.sem, lo_ready.at(b, k))
                    half = P if g in (0, 3) else 0
                    sp.dma_start(qk_parts[bass.ds(b, 1), g // 2, :, half:half + P, :]
                                 .rearrange("o s p t -> p (o s) t"), parts[:, k % 2]) \
                        .then_inc(parts_sent[k % 2].sem, 16)
                sp.wait_ge(v_copied.sem, v_copied.at(b, 1))
                sp.dma_start(v_rows[bass.ds(b, 1)].rearrange("o p f -> (o p) f"),
                             vt[:].rearrange("p g n h w -> p (g n h w)")).then_inc(v_sent.sem, 16)
                sp.wait_ge(r_step.sem, r_step.at(b, 8))
                sp.dma_start(t_parts[bass.ds(b, 1)].rearrange("o r s t -> (o r) s t"), tp[0:2 * N_HYP]) \
                    .then_inc(tp_sent.sem, 16)
                sp.wait_ge(rk_ready.sem, rk_ready.at(b))
                sp.dma_start(rk_cols[bass.ds(b, 1)].rearrange("o p f -> (o p) f"),
                             rk[:].rearrange("p n h -> p (n h)")).then_inc(rk_sent.sem, 16)
            for k in range(2):
                sp.wait_ge(parts_sent[k].sem, parts_sent[k].at(B - 1, 1))
            sp.wait_ge(v_sent.sem, v_sent.at(B - 1))
            sp.wait_ge(tp_sent.sem, tp_sent.at(B - 1))
            sp.wait_ge(rk_sent.sem, rk_sent.at(B - 1))

        @block.tensor
        def _(pe):
            x_turned.start(pe)
            v_ready.start(pe)
            rows_ready.start(pe)
            cols_ready.start(pe)
            pe.wait_ge(consts, 16 * NCONST)
            with pe.Fori(0, B) as b:
                pe.wait_ge(x_here.sem, x_here.at(b))
                def turn_x(c, ps):
                    for n in range(NT):
                        m = pe.transpose(ps[:, n * P:(n + 1) * P], xin[:, n, c * P:(c + 1) * P], ident[:])
                    m.then_inc(x_turned.sem, 1)

                def product(g, swapped, ps):
                    o = (2 * C if swapped else 0) + W_COL[g] * P
                    for c in range(CK):
                        for t in range(0, T, HB):
                            m = pe.matmul(ps[:, t:t + HB], w[:, c, o:o + P], xT[:, c, t:t + HB],
                                          start=(c == 0), stop=(c == CK - 1))
                    m.then_inc(qk_ready.sem, 1)

                def values(half, ps):
                    for n in range(4):
                        tok = (half * 4 + n) * P
                        for c in range(CK):
                            m = pe.matmul(ps[:, n * C:(n + 1) * C], xT[:, c, tok:tok + P], w[:, c, 4 * C:5 * C],
                                          start=(c == 0), stop=(c == CK - 1))
                    m.then_inc(v_ready.sem, 1)

                pe.wait_ge(rk_ready.sem, rk_ready.before(b))
                turn_x(0, slot[0])
                turn_x(1, slot[1])
                pe.wait_ge(xt_ready.sem, xt_ready.at(b, 1))
                product(0, False, slot[2])
                product(0, True, slot[3])
                product(1, False, slot[0])
                product(1, True, slot[1])
                pe.wait_ge(mul_done.sem, mul_done.at(b, 0))
                pe.wait_ge(sq_ready.sem, sq_ready.at(b, 0))
                for t in range(0, T, HB):
                    m = pe.matmul(slot[2][:, t:t + HB], blk[:], sq[:, 0, t:t + HB], start=True, stop=True)
                m.then_inc(norm_ready.sem, 1)
                pe.wait_ge(mul_done.sem, mul_done.at(b, 1))
                product(2, False, slot[3])
                pe.wait_ge(mul_done.sem, mul_done.at(b, 2))
                product(2, True, slot[0])
                pe.wait_ge(mul_done.sem, mul_done.at(b, 3))
                product(3, False, slot[1])
                pe.wait_ge(fac_max.sem, fac_max.at(b))
                product(3, True, slot[2])
                pe.wait_ge(mul_done.sem, mul_done.at(b, 4))
                values(0, slot[3])
                pe.wait_ge(mul_done.sem, mul_done.at(b, 5))
                values(1, slot[0])
                pe.wait_ge(mul_done.sem, mul_done.at(b, 6))
                pe.wait_ge(sq_ready.sem, sq_ready.at(b, G - 1))
                for t in range(0, T, HB):
                    for g in range(G):
                        m = pe.matmul(slot[1][0:16, t:t + HB], rowind[:, g, :], sq[:, g, t:t + HB],
                                      start=(g == 0), stop=(g == G - 1))
                m.then_inc(rows_ready.sem, 1)
                pe.wait_ge(v_copied.sem, v_copied.at(b, 1))
                hold(pe, r_step.sem, r_step.at(b, 3), pe_passed)
                for n in range(NT):
                    m = pe.transpose(slot[0][:, n * 16:(n + 1) * 16], rr[:, n * P:(n + 1) * P], ident[0:16, 0:16])
                m.then_inc(cols_ready.sem, 1)

        @block.scalar
        def _(act):
            act.preload_act_table_set("natural_log_exp_and_others")
            rk_ready.start(act)
            act.wait_ge(consts, 16 * NCONST)
            with act.Fori(0, B) as b:
                act.wait_ge(v_ready.sem, v_ready.before(b, 1))
                for c in range(CK):
                    act.wait_ge(x_turned.sem, x_turned.at(b, c))
                    act.activation(xT[:, c, :], slot[c][:], ACT.Copy).then_inc(xt_ready.sem, 1)
                act.wait_ge(rows_ready.sem, rows_ready.before(b))
                for g in range(G):
                    act.wait_ge(rot_ready.sem, rot_ready.at(b, g))
                    act.activation(sq[:, g, :], rot[:, g, :], ACT.Square).then_inc(sq_ready.sem, 1)
                    if g == 1:
                        act.wait_ge(fac_max.sem, fac_max.at(b))
                        act.activation(fac[:], fac[:], ACT.Ln).then_inc(fac_ln.sem, 1)
                        act.wait_ge(fac_ln.sem, fac_ln.at(b))
                        act.activation(fac[:], fac[:], ACT.Exp, scale=-0.5).then_inc(fac_exp.sem, 1)
                act.wait_ge(ra_ready.sem, ra_ready.at(b))
                act.wait_ge(cols_ready.sem, cols_ready.before(b))
                act.activation(rr[:], ra[:], ACT.Ln).then_inc(r_ln.sem, 1)
                act.wait_ge(r_ln.sem, r_ln.at(b))
                act.activation(rr[:], rr[:], ACT.Exp, scale=-0.5).then_inc(r_exp.sem, 1)
                act.wait_ge(cols_ready.sem, cols_ready.at(b))
                act.wait_ge(rk_sent.sem, rk_sent.before(b))
                act.activation(rk[:], slot[0][:, 0:NT * 16].rearrange("p (n r) -> p n r", r=16)
                               [:, :, 2 * N_HYP:2 * N_HYP + N_COS], ACT.Copy, scale=float(HD) ** 0.5) \
                    .then_inc(rk_ready.sem, 1)

        @block.gpsimd
        def _(pool):
            pool.wait_ge(consts, 16 * NCONST)
            with pool.Fori(0, B) as b:
                for k, g in enumerate(SPLIT):
                    if g == 0:
                        pool.wait_ge(q_scaled.sem, q_scaled.at(b))
                    else:
                        pool.wait_ge(rot_ready.sem, rot_ready.at(b, g))
                    sent = parts_sent[k % 2]
                    hold(pool, sent.sem, sent.before(b, 1) if k < 2 else sent.at(b, 0), pool_passed)
                    pool.tensor_copy(parts[:, k % 2, 0, :], rot[:, g, :]).then_inc(hi_ready.sem, 1)
                    hold(pool, rest_ready.sem, rest_ready.at(b, k), pool_passed)
                    pool.tensor_copy(parts[:, k % 2, 1, :], rest[:]).then_inc(mid_ready.sem, 1)

        @block.vector
        def _(dve):
            lo_ready.start(dve)
            r_step.start(dve)
            rot_ready.start(dve)
            dve.wait_ge(consts, 16 * NCONST)
            dve.tensor_tensor(kfac[:], kcurv[:, :, 1], kcurv[:, :, 0], ALU.subtract).then_inc(setup_dve, 1)
            dve.reciprocal(radd[:, 0:1], rcurv[:, 0:1]).then_inc(setup_dve, 1)
            dve.wait_ge(setup_dve, 2)
            dve.tensor_tensor(radd[:, 1:2], radd[:, 0:1], rcurv[:, 1:2], ALU.mult).then_inc(setup_dve, 1)
            dve.tensor_tensor(radd[:, 2:3], rcurv[:, 0:1], rcurv[:, 2:3], ALU.mult).then_inc(setup_dve, 1)
            for i in range(2):
                dve.tensor_scalar(ktabs[:, i], tabs[:], kfac[:, i:i + 1], None, ALU.mult).then_inc(setup_dve, 1)
            dve.wait_ge(setup_dve, 6)
            dve.tensor_tensor(radd[:, 0:1], radd[:, 1:2], radd[:, 2:3], ALU.add).then_inc(setup_dve, 1)
            dve.wait_ge(setup_dve, 7)
            with dve.Fori(0, B) as b:
                def rotate(g):
                    tab = tabs if g < 2 else ktabs[:, g - 2]
                    ps = (slot[2], slot[3], slot[0], slot[1], slot[3], slot[0], slot[1], slot[2])
                    dve.wait_ge(rot_ready.sem, rot_ready.at(b, g - 1) if g else rot_ready.before(b, G - 1))
                    for i in range(2):
                        dve.wait_ge(qk_ready.sem, qk_ready.at(b, 2 * g + i))
                        dve.tensor_tensor(prod[:, i, :], ps[2 * g + i][:], tab[:, i, :], ALU.mult) \
                            .then_inc(mul_done.sem, 1)
                    dve.wait_ge(mul_done.sem, mul_done.at(b, 2 * g + 1))
                    if g > 0:
                        dve.wait_ge(lo_ready.sem, lo_ready.before(b, SPLIT.index(g)))
                    dve.tensor_tensor(rot[:, g, :], prod[:, 0, :], prod[:, 1, :], ALU.add) \
                        .then_inc(rot_ready.sem, 1)

                def cut(k):
                    g = SPLIT[k]
                    buf = parts[:, k % 2]
                    dve.wait_ge(hi_ready.sem, hi_ready.at(b, k))
                    dve.tensor_tensor(rest[:], rot[:, g, :], buf[:, 0, :], ALU.subtract).then_inc(rest_ready.sem, 1)
                    dve.wait_ge(mid_ready.sem, mid_ready.at(b, k))
                    dve.tensor_tensor(buf[:, 2, :], rest[:], buf[:, 1, :], ALU.subtract).then_inc(lo_ready.sem, 1)
                    dve.wait_ge(lo_ready.sem, lo_ready.at(b, k))

                rotate(0)
                rotate(1)
                cut(0)
                dve.wait_ge(norm_ready.sem, norm_ready.at(b))
                dve.tensor_scalar(fac[:], slot[2][:], TINY, nhyp[:, 0:1], ALU.max, ALU.add).then_inc(fac_max.sem, 1)
                rotate(2)
                dve.wait_ge(fac_exp.sem, fac_exp.at(b))
                dve.wait_ge(sq_ready.sem, sq_ready.at(b, 0))
                dve.wait_ge(rot_ready.sem, rot_ready.at(b, 0))
                dve.tensor_tensor(rot[:, 0, :], rot[:, 0, :], fac[:], ALU.mult).then_inc(q_scaled.sem, 1)
                dve.wait_ge(q_scaled.sem, q_scaled.at(b))
                cut(1)
                rotate(3)
                cut(2)
                for half in range(2):
                    dve.wait_ge(v_ready.sem, v_ready.at(b, half))
                    dve.wait_ge(v_sent.sem, v_sent.before(b))
                    ps = slot[3] if half == 0 else slot[0]
                    for grp in range(4):
                        ins = dve.tensor_copy(
                            vt[:, grp, half * 4:half * 4 + 4, :, 0:HD],
                            ps[:].rearrange("p (n g h d) -> p g n h d", n=4, g=4, h=4)[:, grp])
                    ins.then_inc(v_copied.sem, 1)
                cut(3)
                dve.wait_ge(rows_ready.sem, rows_ready.at(b))
                dve.tensor_scalar(ra[:], slot[1][0:16, :], radd[:, 0:1], TINY, ALU.add, ALU.max) \
                    .then_inc(ra_ready.sem, 1)
                dve.wait_ge(r_exp.sem, r_exp.at(b))

                def step(k, ins):
                    ins.then_inc(r_step.sem, 1)
                    dve.wait_ge(r_step.sem, r_step.at(b, k))

                step(0, dve.tensor_tensor(rt[:], ra[:], rr[:], ALU.mult))
                step(1, dve.tensor_tensor(rt[:], rt[:], rr[:], ALU.mult))
                step(2, dve.tensor_scalar(rt[:], rt[:], -0.5, 1.5, ALU.mult, ALU.add))
                step(3, dve.tensor_tensor(rr[:], rr[:], rt[:], ALU.mult))
                step(4, dve.tensor_tensor(rt[:], ra[:], rr[:], ALU.mult))
                dve.wait_ge(tp_sent.sem, tp_sent.before(b))
                step(5, dve.tensor_copy(tp[:, 0, :], rt[:]))
                step(6, dve.tensor_tensor(ra[:], rt[:], tp[:, 0, :], ALU.subtract))
                step(7, dve.tensor_copy(tp[:, 1, :], ra[:]))
                step(8, dve.tensor_tensor(tp[:, 2, :], ra[:], tp[:, 1, :], ALU.subtract))


def attend(nc, io, qk_parts, t_parts, v_rows, rk_cols, m_parts, x_mid):
    with ExitStack() as ctx:
        def sb(name, shape, dt=F32):
            return ctx.enter_context(nc.sbuf_tensor(name, shape, dt))

        def ev(name, per=1, step=1, carried=False):
            return Event(ctx, nc, name, per, step, carried)

        def sem(name):
            return ctx.enter_context(nc.semaphore(name))

        def psum(name):
            return ctx.enter_context(nc.psum_tensor(name, [P, HB], F32))

        NQ, NSLOT = 36, 4

        def quad(u):
            g, v = divmod(u, 12)
            c, j = (0, v) if v < 4 else (1, v - 4)
            t0 = max(HB * c, P * j)
            return g, c, j, t0, HB * (c + 1) - t0

        def pieces(i):
            w = P * (i + 1)
            return [(s0, min(HB, w - s0)) for s0 in range(0, w, HB)]

        def rows_of(h):
            if h < N_DOT:
                return KR + 3
            return KR + NPAIR if h < COS0 else KR

        NPAIRS = 2 * NT
        ORDER = (1, 0, 3, 2, 5, 7, 6, 4)

        def pair(n):
            i, p = ORDER[n // 2], n % 2
            return i, (HYP0 + 2 * p, HYP0 + 2 * p + 1), P * (i + 1), pieces(i)

        blocks = {n: [(j, k) for j in range(pair(n)[0] + 1) for k in range(2)] for n in range(NPAIRS)}
        turns = {n: [b_[q:q + 4] for q in range(0, len(b_), 4)] for n, b_ in blocks.items()}
        work = [[[] for _ in range(NSLOT)] for _ in range(NQ + 1)]

        def spread(u, items):
            for i, item in enumerate(items):
                work[u][i * NSLOT // len(items)].append(item)

        for u in range(1, NQ + 1):
            work[u][0].append(("values", u - 1))
            if (u - 1) % 12 in (3, 11):
                work[u][u < NQ].append(("sums", 2 * ((u - 1) // 12) + ((u - 1) % 12 == 11)))
        for n in range(NPAIRS):
            spread(max(2 * n - 1, 0), [("argument", n, k, pc) for k in range(2) for pc in range(len(pair(n)[3]))])
            work[2 * n + 1][0].append(("log_square", n))
            work[2 * n + 1][2].append(("root", n))
            work[2 * n + 1][3].append(("add_root", n))
            work[2 * n + 2][0].append(("log_sum", n))
            work[2 * n + 2][1].append(("log_distance", n))
            work[2 * n + 2][2].append(("inverse", n))
            work[2 * n + 2][3].append(("row_bias", n))
            work[2 * n + 3][1].append(("hyp_exp", n, 0))
            work[2 * n + 3][3].append(("hyp_exp", n, 1))
            spread(2 * n + 4, [("turn", n, q) for q in range(len(turns[n]))])
            if n % 2:
                ends = [pair(n)[0] * k // NSLOT + 1 if k else 0 for k in range(NSLOT + 1)]
                for k in range(NSLOT):
                    if ends[k] < ends[k + 1]:
                        work[2 * n + 5][k].append(("hyp_values", n // 2, ends[k], ends[k + 1]))
                work[2 * n + 5][NSLOT - 1].append(("hyp_sums", n // 2))
        ALL_MAX = [(h, i, pc, s0, w) for h in range(N_DOT) for i in range(NT) for pc, (s0, w) in enumerate(pieces(i))]
        MAX_STEPS = 9
        for u in range(MAX_STEPS):
            spread(u, [("maximum", m) for m in range(len(ALL_MAX)) if m * MAX_STEPS // len(ALL_MAX) == u])
        work[MAX_STEPS][1].append(("join_maxima",))
        work[MAX_STEPS][3].append(("turn_maxima",))
        for n in range(NT):
            work[10 + 2 * n][1].append(("turn_rows", n))
            work[11 + 2 * n][1].append(("project", n))
            work[12 + 2 * n][2].append(("statistics", 0, n, n + 1))
            work[29 + n if n < NT // 2 else n - NT // 2][1].append(("turn_sums", n))
        work[27][0].append(("variance", 0))
        work[27][3].append(("inverse_root", 0))
        work[28][1].append(("normalize", 0))
        work[29][2].append(("add_bias",))
        work[30][1].append(("statistics", 1, 0, NT // 2))
        work[30][3].append(("statistics", 1, NT // 2, NT))
        work[31][1].append(("variance", 1))
        work[31][3].append(("inverse_root", 1))
        work[32][1].append(("normalize", 1))
        RINGED = ("argument", "maximum", "turn_maxima", "turn_rows", "project", "turn_sums", "turn")
        ringed = [item for step in work for slot in step for item in slot if item[0] in RINGED]
        WB = 3
        MORE = -len(ringed) % WB
        n_wide = len(ringed) + MORE
        m_item = ringed.index(("turn_maxima",))
        wide = {item: x + MORE * (x > m_item) for x, item in enumerate(ringed)}
        last_argument = [item for item in ringed if item[0] == "argument"][-1]
        last_max = ("maximum", len(ALL_MAX) - 1)
        LATE = ("turn_rows", "project", "statistics", "variance", "inverse_root", "normalize", "add_bias")

        def is_late(item):
            return item[0] in LATE or item[0] == "turn_sums" and item[1] >= NT // 2

        tail = [("turn_sums", n) for n in range(NT // 2, NT)] + [("turn_rows", 0)]
        for n in range(NT):
            tail += [("turn_rows", n + 1)] * (n + 1 < NT) + [("project", n), ("statistics", 0, n, n + 1)]
        tail += [("variance", 0), ("inverse_root", 0), ("normalize", 0), ("add_bias",), ("statistics", 1, 0, NT),
                 ("variance", 1), ("inverse_root", 1), ("normalize", 1)]
        tail_wide = {item: x for x, item in enumerate([it for it in tail if it[0] in RINGED])}
        RB = 3

        def last_turn(n):
            return wide["turn", n, len(turns[n]) - 1]

        def r_before(n):
            if n >= RB:
                return n - RB, False
            return max(m for m in range(NPAIRS) if m % RB == n % RB), True

        ident = sb("a_ident", [P, P])
        identb = sb("a_identb", [P, P], BF16)
        masks = sb("a_masks", [P, 4, P])
        masksb = sb("a_masksb", [P, 3, P], BF16)
        curv = sb("a_curv", [P, N_HYP])
        root = sb("a_root", [P, 4, N_HYP])
        wproj = sb("a_wproj", [P, CK, C])
        bias = sb("a_bias", [1, C])
        ones = sb("a_ones", [1, P])
        bias2 = sb("a_bias2", [P, C])
        Qb = sb("a_Q", [P, H, T], BF16)
        Kb = sb("a_K", [P, H, T], BF16)
        V = sb("a_V", [P, 4, NT, 4, VW])
        rk = sb("a_rk", [P, NT, N_COS])
        PT = sb("a_PT", [P, 2, 4, HB])
        mx = sb("a_mx", [P, 2, N_DOT * NT])
        mrow = sb("a_mrow", [N_DOT * NT, 2, P])
        mpart = sb("a_mpart", [N_DOT * NT, 3, P], BF16)
        ZW = T + 2
        Z = sb("a_Z", [P, 2, 2, ZW])
        R = sb("a_R", [P, RB, 2, ZW])
        nb = sb("a_nb", [P, 2, 2, 2])
        PTh = sb("a_PTh", [P, NT, 4, P])
        O = sb("a_O", [P, 4, T])
        X = sb("a_X", [P, NT, C])
        X3 = sb("a_X3", [P, NT, C])
        Y = sb("a_Y", [P, NT, H, HD])
        rden = sb("a_rden", [P, 2, H])
        YT = sb("a_YT", [P, 2, CK, P])
        st = sb("a_st", [P, NT, 6])
        mv = sb("a_mv", [P, NT, 2])
        rs = sb("a_rs", [P, 3, NT])
        sB = [psum(f"a_s{i}") for i in range(3)]
        oB = psum("a_o")
        wB = [psum(f"a_w{i}") for i in range(WB)]
        oH = psum("a_oh")

        consts, setup, act_setup = sem("a_consts"), sem("a_setup"), sem("a_act_setup")
        dve_passed, pool_passed, sp_passed = sem("a_dve_passed"), sem("a_pool_passed"), sem("a_sp_passed")
        NCONST = 7
        NLOAD = {0: 12, 1: 12, 2: 24, 3: 24}
        qk_here = {g: ev(f"a_qk_here{g}", 1, 16 * NLOAD[g]) for g in range(4)}
        m_sent, m_here = ev("a_m_sent", 1, 16), ev("a_m_here", 1, 16 * N_DOT)
        v_here = {g: ev(f"a_v_here{g}", 1, 16) for g in range(4)}
        rk_here, x_here = ev("a_rk_here", 1, 16), ev("a_x_here", 1, 16)
        score = ev("a_score", NQ * 4, carried=True)
        prob = ev("a_prob", NQ * 4, carried=True)
        valued = ev("a_valued", NQ, carried=True)
        o_copied = ev("a_o_copied", 6, carried=True)
        wide_full, wide_free = ev("a_wide_full", n_wide, carried=True), ev("a_wide_free", n_wide, carried=True)
        m_step = ev("a_m_step", 6)
        z_sq = ev("a_z_sq", NPAIRS)
        z_ln, z_root = ev("a_z_ln", NPAIRS), ev("a_z_root", NPAIRS)
        z_sum = ev("a_z_sum", NPAIRS)
        d_ln, d_ln2 = ev("a_d_ln", NPAIRS), ev("a_d_ln2", 2 * NPAIRS)
        d_inv = ev("a_d_inv", NPAIRS, carried=True)
        b_max, b_ready = ev("a_b_max", NPAIRS), ev("a_b_ready", NPAIRS)
        h_prob = ev("a_h_prob", 2 * NPAIRS)
        h_valued, h_copied = ev("a_h_valued", NT, carried=True), ev("a_h_copied", NT, carried=True)
        y_inv, stats = ev("a_y_inv", NT), ev("a_stats", 4 * NT)
        var_ready, rs_ln, rs_exp = ev("a_var", 2), ev("a_rs_ln", 2), ev("a_rs_exp", 2)
        rs_step, normed = ev("a_rs_step", 8), ev("a_normed", 2)
        biased = ev("a_biased")
        mid_sent, out_sent = ev("a_mid_sent", 1, 16), ev("a_out_sent", 1, 16)
        x3_sent = ev("a_x3_sent", carried=True)
        block = ctx.enter_context(nc.Block())

        @block.sync
        def _(sp):
            for dst, name in ((ident, "ident"), (masks, "masks"), (curv, "acurv"), (wproj, "w_proj"),
                              (bias, "proj_b"), (bias2, "ffn_b")):
                sp.dma_start(dst[:], io[name]).then_inc(consts, 16)
            sp.dma_start(root[:, 0], io["acurv"]).then_inc(consts, 16)
            with sp.Fori(0, B) as b:
                def heads(g, runs):
                    for qk, buf, order in ((0, Qb, QPART), (1, Kb, KPART)):
                        for r, part in enumerate(order):
                            for h0, h1 in runs:
                                src = qk_parts[bass.ds(b, 1), qk, part, h0 * HD:h1 * HD, :]
                                sp.dma_start(buf[r * HD:(r + 1) * HD, h0:h1, :],
                                             src.rearrange("o (h d) t -> d (o h) t", d=HD)) \
                                    .then_inc(qk_here[g].sem, 16)

                def values(g):
                    sp.dma_start(V[:, g].rearrange("p n h w -> p (n h w)"),
                                 v_rows[bass.ds(b, 1), :, g * NT * 4 * VW:(g + 1) * NT * 4 * VW]
                                 .rearrange("o p f -> (o p) f")).then_inc(v_here[g].sem, 16)

                def inverse_norms():
                    sp.dma_start(rk[:].rearrange("p n h -> p (n h)"),
                                 rk_cols[bass.ds(b, 1)].rearrange("o p f -> (o p) f")).then_inc(rk_here.sem, 16)

                sp.wait_ge(valued.sem, valued.before(b, 11))
                heads(0, ((12, 16),))
                values(0)
                hold(sp, valued.sem, valued.before(b, 23), sp_passed)
                heads(1, ((0, 4),))
                values(1)
                hold(sp, wide_full.sem, wide_full.before(b, wide[last_argument]), sp_passed)
                heads(3, ((HYP0, COS0),))
                for i in range(NPAIR):
                    for buf, first, order in ((Qb, 0, QPART), (Kb, N_HYP, KPART)):
                        sp.dma_start(buf[KR + i:KR + i + 1, HYP0:COS0, :],
                                     t_parts[bass.ds(b, 1), first:first + N_HYP, order[i], :]) \
                            .then_inc(qk_here[3].sem, 16)
                sp.wait_ge(prob.sem, prob.before(b, 4 * NQ - 1))
                inverse_norms()
                hold(sp, valued.sem, valued.before(b, NQ - 1), sp_passed)
                heads(2, ((4, 6), (10, 12)))
                values(2)
                sp.wait_ge(h_valued.sem, h_valued.before(b, NT - 1))
                values(3)
                sp.wait_ge(m_step.sem, m_step.at(b, 5))
                sp.dma_start(m_parts, mpart[:]).then_inc(m_sent.sem, 16)
                sp.wait_ge(m_sent.sem, m_sent.at(b))
                for h in range(N_DOT):
                    sp.dma_start(Qb[KR:KR + 3, h, :].rearrange("r (i c) -> r i c", c=P),
                                 m_parts[h * NT:(h + 1) * NT].rearrange("i r c -> r i c")).then_inc(m_here.sem, 16)

        @block.tensor
        def _(pe):
            for e in (score, valued, wide_full, h_valued):
                e.start(pe)
            pe.wait_ge(consts, 16 * NCONST)
            pe.wait_ge(setup, 4)

            def scores(b, u, k):
                g, c, j, t0, w = quad(u)
                h, x = GROUPS[g][k], 4 * u + k
                pe.wait_ge(prob.sem, prob.at(b, x - 3) if x >= 3 else prob.before(b, 4 * NQ - 3 + x))
                bank, r = sB[x % 3], rows_of(h)
                diag = t0 == P * j
                m = pe.matmul(bank[:, 0:w], Kb[0:r, h, P * j:P * j + P], Qb[0:r, h, t0:t0 + w],
                              start=True, stop=not diag)
                if diag:
                    m = pe.matmul(bank[:, 0:P], identb[:], masksb[:, 0, :], start=False, stop=True)
                m.then_inc(score.sem, 1)

            def apply_values(b, u):
                g, c, j, t0, w = quad(u)
                pe.wait_ge(prob.sem, prob.at(b, 4 * u + 3))
                if j == 0:
                    n = 2 * g + c
                    pe.wait_ge(o_copied.sem, o_copied.at(b, n - 1) if n else o_copied.before(b, 5))
                    pe.wait_ge(v_here[g].sem, v_here[g].at(b))
                for k in range(4):
                    m = pe.matmul(oB[VW * k:VW * k + VW, t0 - HB * c:t0 - HB * c + w], V[:, g, j, k, :],
                                  PT[:, u % 2, k, 0:w], start=(j == 0), stop=(j == 4 * c + 3))
                m.then_inc(valued.sem, 1)

            def wide_bank(b, x):
                pe.wait_ge(wide_free.sem, wide_free.at(b, x - WB) if x >= WB else wide_free.before(b, n_wide - WB + x))
                return wB[x % WB]

            def row_scores(b, x, h, i, s0, w, mask):
                bank = wide_bank(b, x)
                diag = s0 + w == P * (i + 1)
                r = KR if h < N_DOT else rows_of(h)
                m = pe.matmul(bank[:, 0:w], Qb[0:r, h, P * i:P * i + P], Kb[0:r, h, s0:s0 + w],
                              start=True, stop=not diag)
                if diag:
                    m = pe.matmul(bank[:, w - P:w], identb[:], masksb[:, mask, :], start=False, stop=True)
                m.then_inc(wide_full.sem, 1)

            def turn_pair(b, n, q):
                if q == 0:
                    pe.wait_ge(h_prob.sem, h_prob.at(b, 2 * n + 1))
                bank = wide_bank(b, wide["turn", n, q])
                for a, (j, k) in enumerate(turns[n][q]):
                    m = pe.transpose(bank[:, a * P:(a + 1) * P], R[:, n % RB, k, P * j:P * j + P], ident[:])
                m.then_inc(wide_full.sem, 1)

            def apply_hyp_values(b, e, j0, j1):
                i, o = ORDER[e], P * (e % 4)
                if j0 == 0:
                    pe.wait_ge(wide_free.sem, wide_free.at(b, last_turn(2 * e + 1)))
                    pe.wait_ge(h_copied.sem, h_copied.at(b, e - 1) if e else h_copied.before(b, NT - 1))
                    if e == 0:
                        pe.wait_ge(v_here[3].sem, v_here[3].at(b))
                for j in range(j0, j1):
                    for k in range(4):
                        m = pe.matmul(oH[VW * k:VW * k + VW, o:o + P], V[:, 3, j, k, :], PTh[:, j, k, :],
                                      start=(j == 0), stop=(j == i))
                if j1 == i + 1:
                    m.then_inc(h_valued.sem, 1)

            def turn_sums(b, d, n, x):
                bank = wide_bank(b, x)
                pe.wait_ge(o_copied.sem, o_copied.at(d, 4 if n < NT // 2 else 5))
                pe.wait_ge(h_copied.sem, h_copied.at(d, ORDER.index(n)))
                for g in range(4):
                    m = pe.transpose(bank[:, g * P:(g + 1) * P], O[:, g, n * P:(n + 1) * P], ident[:])
                m.then_inc(wide_full.sem, 1)

            def turn_rows(b, n, x):
                bank = wide_bank(b, x)
                for c in range(CK):
                    m = pe.transpose(bank[:, c * P:(c + 1) * P],
                                     Y[:, n].rearrange("p h d -> p (h d)")[:, c * P:(c + 1) * P], ident[:])
                m.then_inc(wide_full.sem, 1)

            def project_rows(b, n, index):
                x, turned = index["project", n], index["turn_rows", n]
                if turned > x - WB:
                    pe.wait_ge(wide_free.sem, wide_free.at(b, turned))
                    bank = wB[x % WB]
                else:
                    bank = wide_bank(b, x)
                for c in range(CK):
                    pe.matmul(bank[:, 0:C], YT[:, n % 2, c, :], wproj[:, c, :], start=(c == 0), stop=False)
                pe.matmul(bank[:, 0:C], ones[:], bias[:], start=False, stop=True).then_inc(wide_full.sem, 1)

            def late(b, d, item, index):
                if item[0] == "turn_sums":
                    turn_sums(b, d, item[1], index[item])
                elif item[0] == "turn_rows":
                    turn_rows(b, item[1], index[item])
                else:
                    project_rows(b, item[1], index)

            def do(b, item):
                kind = item[0]
                if kind == "values":
                    apply_values(b, item[1])
                elif kind == "argument":
                    _, n, k, pc = item
                    i, hs, _, pcs = pair(n)
                    if n == 0 and k == 0:
                        pe.wait_ge(qk_here[3].sem, qk_here[3].at(b))
                    row_scores(b, wide[item], hs[k], i, *pcs[pc], 2)
                elif kind == "maximum":
                    h, i, pc, s0, w = ALL_MAX[item[1]]
                    if (i, pc) == (0, 0) and h in (0, 4):
                        g = 1 if h == 0 else 2
                        pe.wait_ge(qk_here[g].sem, qk_here[g].at(b))
                    row_scores(b, wide[item], h, i, s0, w, 1)
                elif kind == "turn_maxima":
                    bank = wide_bank(b, wide[item])
                    pe.wait_ge(m_step.sem, m_step.at(b, 1))
                    pe.transpose(bank[0:N_DOT * NT, 0:P], mx[:, 0, :], ident[:]).then_inc(wide_full.sem, 1 + MORE)
                elif kind == "turn":
                    turn_pair(b, item[1], item[2])
                elif kind == "hyp_values":
                    apply_hyp_values(b, *item[1:])
                elif kind == "turn_sums":
                    turn_sums(b, b, item[1], wide[item])

            def turn(b, first=False):
                for u, step in enumerate(work):
                    for k, slot in enumerate(step):
                        if u < NQ:
                            if k == 0 and u == 0:
                                pe.wait_ge(qk_here[0].sem, qk_here[0].at(b))
                            if k == 0 and u == 12:
                                pe.wait_ge(m_here.sem, m_here.at(b))
                            scores(b, u, k)
                        for item in slot:
                            if is_late(item) and item[0] in RINGED:
                                if first:
                                    wide_bank(b, wide[item])
                                    pe.wait_ge(wide_full.sem, wide_full.at(b, wide[item] - 1))
                                    pe.sem_inc(wide_full.sem, 1)
                                else:
                                    late(b, b - 1, item, wide)
                            else:
                                do(b, item)

            turn(0, first=True)
            with pe.Fori(1, B) as b:
                turn(b)
            for item in tail:
                if item[0] in RINGED:
                    late(B, B - 1, item, tail_wide)

        @block.scalar
        def _(act):
            act.preload_act_table_set("natural_log_exp_and_others")
            prob.start(act)
            d_inv.start(act)
            act.wait_ge(consts, 16 * NCONST)
            act.activation(root[:, 0], curv[:], ACT.Ln).then_inc(act_setup, 1)
            act.wait_ge(act_setup, 1)
            act.activation(root[:, 0], root[:, 0], ACT.Exp, scale=0.5).then_inc(act_setup, 1)
            act.wait_ge(setup, 8)

            def exponentials(b, u, k):
                g, c, j, t0, w = quad(u)
                h, x = GROUPS[g][k], 4 * u + k
                act.wait_ge(valued.sem, valued.at(b, u - 2) if u >= 2 else valued.before(b, NQ - 2 + u))
                act.wait_ge(score.sem, score.at(b, x))
                scale = rk[:, j, h - COS0:h - COS0 + 1] if h >= COS0 else float(HD) ** -0.5
                act.activation(PT[:, u % 2, k, 0:w], sB[x % 3][:, 0:w], ACT.Exp, scale=scale).then_inc(prob.sem, 1)

            def do(b, item):
                kind, n = item[0], item[1] if len(item) > 1 else None
                if kind in ("log_square", "root", "log_sum", "log_distance", "inverse", "hyp_exp"):
                    _, hs, w, pcs = pair(n)
                    ww = w + len(pcs)
                    z, r = Z[:, n % 2, :, 0:ww], R[:, n % RB, :, 0:ww]
                if kind == "log_square":
                    act.wait_ge(z_sq.sem, z_sq.at(b, n))
                    act.activation(r, r, ACT.Ln, bias=-1.0).then_inc(z_ln.sem, 1)
                elif kind == "root":
                    act.wait_ge(z_ln.sem, z_ln.at(b, n))
                    act.activation(r, r, ACT.Exp, scale=0.5).then_inc(z_root.sem, 1)
                elif kind == "log_sum":
                    act.wait_ge(z_sum.sem, z_sum.at(b, n))
                    act.activation(r, z, ACT.Ln).then_inc(d_ln.sem, 1)
                elif kind == "log_distance":
                    act.wait_ge(d_ln.sem, d_ln.at(b, n))
                    for k, h in enumerate(hs):
                        act.activation(Z[:, n % 2, k, 0:ww], R[:, n % RB, k, 0:ww], ACT.Ln,
                                       bias=root[:, 3, h - HYP0:h - HYP0 + 1]).then_inc(d_ln2.sem, 1)
                elif kind == "inverse":
                    act.wait_ge(d_ln2.sem, d_ln2.at(b, 2 * n + 1))
                    act.activation(r, z, ACT.Exp, scale=-1.0).then_inc(d_inv.sem, 1)
                elif kind == "hyp_exp":
                    k = item[2]
                    if k == 0:
                        act.wait_ge(b_ready.sem, b_ready.at(b, n))
                    act.activation(R[:, n % RB, k, 0:w], R[:, n % RB, k, 0:w], ACT.Exp,
                                   scale=root[:, 0, hs[k] - HYP0:hs[k] - HYP0 + 1],
                                   bias=nb[:, n % 2, 1, k:k + 1]).then_inc(h_prob.sem, 1)

            def inverse_root(d, a):
                act.wait_ge(var_ready.sem, var_ready.at(d, a))
                act.activation(rs[:, 1], rs[:, 0], ACT.Ln).then_inc(rs_ln.sem, 1)
                act.wait_ge(rs_ln.sem, rs_ln.at(d, a))
                act.activation(rs[:, 1], rs[:, 1], ACT.Exp, scale=-0.5).then_inc(rs_exp.sem, 1)

            def turn(b, first=False):
                for u, step in enumerate(work):
                    for k, slot in enumerate(step):
                        if u < NQ:
                            if k == 0 and u == 0:
                                act.wait_ge(rk_here.sem, rk_here.at(b))
                            exponentials(b, u, k)
                        for item in slot:
                            if item[0] not in LATE:
                                do(b, item)
                            elif item[0] == "inverse_root" and not first:
                                inverse_root(b - 1, item[1])

            turn(0, first=True)
            with act.Fori(1, B) as b:
                turn(b)
            for a in range(2):
                inverse_root(B - 1, a)

        @block.gpsimd
        def _(pool):
            def squares(b):
                for n in range(NPAIRS):
                    _, _, w, pcs = pair(n)
                    ww = w + len(pcs)
                    pool.wait_ge(wide_free.sem, wide_free.at(b, wide["argument", n, 1, len(pcs) - 1]))
                    m, earlier = r_before(n)
                    pool.wait_ge(wide_full.sem, (wide_full.before if earlier else wide_full.at)(b, last_turn(m)))
                    pool.tensor_tensor(R[:, n % RB, :, 0:ww], Z[:, n % 2, :, 0:ww], Z[:, n % 2, :, 0:ww], ALU.mult) \
                        .then_inc(z_sq.sem, 1)

            def rows_out(d):
                for a, (dram, rows, sent) in enumerate(((x_mid, X, mid_sent), (io["out"], X3, out_sent))):
                    hold(pool, normed.sem, normed.at(d, a), pool_passed)
                    pool.dma_start(dram[bass.ds(d, 1)].rearrange("o (n p) c -> p (o n) c", p=P), rows[:]) \
                        .then_inc(sent.sem, 16)

            def rows_in(b):
                pool.dma_start(X[:], io["x"][bass.ds(b, 1)].rearrange("o (n p) c -> p (o n) c", p=P)) \
                    .then_inc(x_here.sem, 16)

            x3_sent.start(pool)
            squares(0)
            rows_in(0)
            with pool.Fori(1, B) as b:
                squares(b)
                rows_out(b - 1)
                hold(pool, mid_sent.sem, mid_sent.at(b - 1), pool_passed)
                rows_in(b)
                hold(pool, out_sent.sem, out_sent.at(b - 1), x3_sent.sem)
            rows_out(B - 1)
            pool.wait_ge(mid_sent.sem, mid_sent.at(B - 1))
            pool.wait_ge(out_sent.sem, out_sent.at(B - 1))

        @block.vector
        def _(dve):
            for e in (wide_free, o_copied, h_copied):
                e.start(dve)
            dve.memset(Kb[KR:KR + 3, 0:N_DOT, :], 1.0).then_inc(setup, 1)
            dve.memset(ones[:], 1.0).then_inc(setup, 1)
            dve.memset(mx[:], -3.0e38).then_inc(setup, 1)
            dve.wait_ge(consts, 16 * NCONST)
            dve.wait_ge(setup, 3)
            dve.tensor_copy(identb[:], ident[:])
            dve.tensor_copy(masksb[:], masks[:, 1:4, :]).then_inc(setup, 1)
            dve.wait_ge(act_setup, 2)
            dve.reciprocal(root[:, 1], root[:, 0]).then_inc(setup, 1)
            dve.wait_ge(setup, 5)
            dve.tensor_tensor(root[:, 1], root[:, 1], curv[:], ALU.mult).then_inc(setup, 1)
            dve.wait_ge(setup, 6)
            dve.tensor_tensor(root[:, 1], root[:, 1], root[:, 0], ALU.add).then_inc(setup, 1)
            dve.wait_ge(setup, 7)
            dve.tensor_scalar(root[:, 2], root[:, 1], -0.5, None, ALU.mult)
            dve.tensor_scalar(root[:, 3], root[:, 1], 0.5e-6, None, ALU.mult)
            dve.tensor_scalar(root[:, 0], root[:, 1], 0.5, None, ALU.mult).then_inc(setup, 1)
            dve.wait_ge(setup, 8)

            def clamp(b, n, k, pc):
                _, _, w, pcs = pair(n)
                s0, pw = pcs[pc]
                x = wide["argument", n, k, pc]
                if k == 0 and pc == 0:
                    dve.wait_ge(d_inv.sem, d_inv.at(b, n - 2) if n >= 2 else d_inv.before(b, NPAIRS - 2 + n))
                dve.wait_ge(wide_full.sem, wide_full.at(b, x))
                dve.tensor_scalar(Z[:, n % 2, k, s0:s0 + pw], wB[x % WB][:, 0:pw],
                                  float(np.float32(1.0 + 1e-7)), 3.0e38, ALU.max, ALU.min,
                                  accum_out=Z[:, n % 2, k, w + pc:w + pc + 1]).then_inc(wide_free.sem, 1)

            def row_maximum(b, m):
                h, i, pc, s0, w = ALL_MAX[m]
                x, col = wide["maximum", m], h * NT + i
                dve.wait_ge(wide_full.sem, wide_full.at(b, x))
                dve.tensor_reduce(mx[:, pc, col:col + 1], wB[x % WB][:, 0:w], AX.X, ALU.max).then_inc(wide_free.sem, 1)

            def join_maxima(b):
                dve.wait_ge(wide_free.sem, wide_free.at(b, wide[last_max]))
                dve.tensor_tensor(mx[:, 0, :], mx[:, 0, :], mx[:, 1, :], ALU.max).then_inc(m_step.sem, 1)
                dve.wait_ge(m_step.sem, m_step.at(b, 0))
                dve.tensor_scalar(mx[:, 0, :], mx[:, 0, :], -1.0, None, ALU.mult).then_inc(m_step.sem, 1)

            def cut_maxima(b):
                x = wide["turn_maxima",]
                dve.wait_ge(wide_full.sem, wide_full.at(b, x + MORE))
                dve.tensor_copy(mrow[:, 0, :], wB[x % WB][0:N_DOT * NT, 0:P]).then_inc(wide_free.sem, 1 + MORE)
                dve.wait_ge(wide_free.sem, wide_free.at(b, x + MORE))
                dve.tensor_copy(mpart[:, 0, :], mrow[:, 0, :]).then_inc(m_step.sem, 1)
                dve.wait_ge(m_step.sem, m_step.at(b, 2))
                dve.tensor_tensor(mrow[:, 1, :], mrow[:, 0, :], mpart[:, 0, :], ALU.subtract).then_inc(m_step.sem, 1)
                dve.wait_ge(m_step.sem, m_step.at(b, 3))
                dve.tensor_copy(mpart[:, 1, :], mrow[:, 1, :]).then_inc(m_step.sem, 1)
                dve.wait_ge(m_step.sem, m_step.at(b, 4))
                dve.tensor_tensor(mpart[:, 2, :], mrow[:, 1, :], mpart[:, 1, :], ALU.subtract).then_inc(m_step.sem, 1)

            def add_root(b, n):
                _, _, w, pcs = pair(n)
                ww = w + len(pcs)
                z = Z[:, n % 2, :, 0:ww]
                dve.wait_ge(z_root.sem, z_root.at(b, n))
                dve.tensor_tensor(z, z, R[:, n % RB, :, 0:ww], ALU.add).then_inc(z_sum.sem, 1)

            def row_bias(b, n):
                _, hs, w, pcs = pair(n)
                k = hs[0] - HYP0
                dve.wait_ge(d_inv.sem, d_inv.at(b, n))
                dve.tensor_tensor(nb[:, n % 2, 0, :], R[:, n % RB, :, w], R[:, n % RB, :, w + len(pcs) - 1],
                                  ALU.max).then_inc(b_max.sem, 1)
                dve.wait_ge(b_max.sem, b_max.at(b, n))
                dve.tensor_tensor(nb[:, n % 2, 1, :], nb[:, n % 2, 0, :], root[:, 2, k:k + 2], ALU.mult) \
                    .then_inc(b_ready.sem, 1)

            def copy_turned(b, n, q):
                e, p = divmod(n, 2)
                i, x = ORDER[e], wide["turn", n, q]
                bank = wB[x % WB]
                if p == 0 and q == 0:
                    dve.wait_ge(h_valued.sem, h_valued.at(b, e - 1) if e else h_valued.before(b, NT - 1))
                dve.wait_ge(wide_full.sem, wide_full.at(b, x))
                js = [j for j, k in turns[n][q] if k == 0]
                below = [j for j in js if j < i]
                if below:
                    nb_ = len(below)
                    ins = dve.tensor_copy(PTh[:, below[0]:below[0] + nb_, 2 * p:2 * p + 2, :],
                                          bank[:, 0:nb_ * 2 * P].rearrange("p (j k t) -> p j k t", j=nb_, k=2))
                    if js[-1] != i:
                        ins.then_inc(wide_free.sem, 1)
                if js[-1] == i:
                    o = 2 * P * len(below)
                    dve.tensor_tensor(PTh[:, i, 2 * p:2 * p + 2, :],
                                      bank[:, o:o + 2 * P].rearrange("p (k t) -> p k t", k=2),
                                      masks[:, 0:1, :].to_broadcast([P, 2, P]), ALU.mult).then_inc(wide_free.sem, 1)

            def copy_hyp_sums(b, e):
                dve.wait_ge(h_valued.sem, h_valued.at(b, e))
                i, o = ORDER[e], P * (e % 4)
                dve.tensor_copy(O[:, 3, P * i:P * i + P], oH[:, o:o + P]).then_inc(h_copied.sem, 1)

            def copy_sums(b, m):
                g, c = divmod(m, 2)
                dve.wait_ge(valued.sem, valued.at(b, 12 * g + (3 if c == 0 else 11)))
                dve.tensor_copy(O[:, g, HB * c:HB * c + HB], oB[:]).then_inc(o_copied.sem, 1)

            def divide_sums(b, d, n, x):
                sums = wB[x % WB][:].rearrange("p (h w) -> p h w", w=VW)
                dve.wait_ge(wide_full.sem, wide_full.at(b, x))
                dve.reciprocal(rden[:, n % 2, :], sums[:, :, HD]).then_inc(y_inv.sem, 1)
                dve.wait_ge(y_inv.sem, y_inv.at(d, n))
                dve.tensor_tensor(Y[:, n], sums[:, :, 0:HD],
                                  rden[:, n % 2, :].unsqueeze(2).to_broadcast([P, H, HD]), ALU.mult) \
                    .then_inc(wide_free.sem, 1)

            def copy_rows(b, d, n, x):
                dve.wait_ge(wide_full.sem, wide_full.at(b, x))
                dve.tensor_copy(YT[:, n % 2].rearrange("p c t -> p (c t)"), wB[x % WB][:, 0:C]).then_inc(wide_free.sem, 1)

            def residual(b, d, n, x):
                if n == 0:
                    dve.wait_ge(x_here.sem, x_here.at(d))
                dve.wait_ge(wide_full.sem, wide_full.at(b, x))
                dve.tensor_tensor(X[:, n, :], X[:, n, :], wB[x % WB][:, 0:C], ALU.add).then_inc(wide_free.sem, 1)

            def late(b, d, item, index):
                x = index.get(item)
                kind = item[0]
                if kind == "turn_sums":
                    divide_sums(b, d, item[1], x)
                elif kind == "turn_rows":
                    copy_rows(b, d, item[1], x)
                elif kind == "project":
                    residual(b, d, item[1], x)
                elif kind == "statistics":
                    _, a, n0, n1 = item
                    if a == 0:
                        dve.wait_ge(wide_free.sem, wide_free.at(b, index["project", n1 - 1]))
                    else:
                        dve.wait_ge(biased.sem, biased.at(d))
                    for n in range(n0, n1):
                        dve.bn_stats(st[:, n, :], (X3 if a else X)[:, n, :]).then_inc(stats.sem, 1)
                elif kind == "variance":
                    a = item[1]
                    hold(dve, stats.sem, stats.at(d, 2 * NT * a + NT - 1), dve_passed)
                    for n in range(NT):
                        dve.bn_aggr(mv[:, n, :], st[:, n, :]).then_inc(stats.sem, 1)
                    dve.wait_ge(stats.sem, stats.at(d, 2 * NT * (a + 1) - 1))
                    dve.tensor_scalar(rs[:, 0], mv[:, :, 1], 1e-5, None, ALU.add).then_inc(var_ready.sem, 1)
                elif kind == "normalize":
                    a = item[1]
                    rows = X3 if a else X
                    dve.wait_ge(rs_exp.sem, rs_exp.at(d, a))

                    def step(k, ins):
                        ins.then_inc(rs_step.sem, 1)
                        dve.wait_ge(rs_step.sem, rs_step.at(d, 4 * a + k))

                    step(0, dve.tensor_tensor(rs[:, 2], rs[:, 0], rs[:, 1], ALU.mult))
                    step(1, dve.tensor_tensor(rs[:, 2], rs[:, 2], rs[:, 1], ALU.mult))
                    step(2, dve.tensor_scalar(rs[:, 2], rs[:, 2], -0.5, 1.5, ALU.mult, ALU.add))
                    step(3, dve.tensor_tensor(rs[:, 1], rs[:, 1], rs[:, 2], ALU.mult))
                    for n in range(NT):
                        ins = dve.tensor_scalar(rows[:, n, :], rows[:, n, :], mv[:, n, 0:1], rs[:, 1, n:n + 1],
                                                ALU.subtract, ALU.mult)
                    ins.then_inc(normed.sem, 1)
                elif kind == "add_bias":
                    dve.wait_ge(normed.sem, normed.at(d, 0))
                    dve.tensor_tensor(X3[:], X[:], bias2[:].unsqueeze(1).to_broadcast([P, NT, C]), ALU.add) \
                        .then_inc(biased.sem, 1)

            def out_free(b):
                dve.wait_ge(x3_sent.sem, x3_sent.before(b - 1))

            def do(b, item):
                kind = item[0]
                if kind == "argument":
                    clamp(b, *item[1:])
                elif kind == "maximum":
                    row_maximum(b, item[1])
                elif kind == "join_maxima":
                    join_maxima(b)
                elif kind == "turn_maxima":
                    cut_maxima(b)
                elif kind == "add_root":
                    add_root(b, item[1])
                elif kind == "row_bias":
                    row_bias(b, item[1])
                elif kind == "turn":
                    copy_turned(b, item[1], item[2])
                elif kind == "hyp_sums":
                    copy_hyp_sums(b, item[1])
                elif kind == "sums":
                    copy_sums(b, item[1])
                elif kind == "turn_sums":
                    divide_sums(b, b, item[1], wide[item])

            def turn(b, first=False):
                for step in work:
                    for slot in step:
                        for item in slot:
                            if not is_late(item):
                                do(b, item)
                            elif not first:
                                if item[0] == "add_bias":
                                    out_free(b)
                                late(b, b - 1, item, wide)
                            elif item[0] in RINGED:
                                dve.wait_ge(wide_full.sem, wide_full.at(b, wide[item]))
                                dve.wait_ge(wide_free.sem, wide_free.at(b, wide[item] - 1))
                                dve.sem_inc(wide_free.sem, 1)

            turn(0, first=True)
            with dve.Fori(1, B) as b:
                turn(b)
            for item in tail:
                if item[0] == "add_bias":
                    out_free(B)
                if item[0] != "inverse_root":
                    late(B, B - 1, item, tail_wide)


def experts(nc, io, x_mid):
    with ExitStack() as ctx:
        def sb(name, shape, dt=F32):
            return ctx.enter_context(nc.sbuf_tensor(name, shape, dt))

        def ev(name, per=1, step=1, carried=False):
            return Event(ctx, nc, name, per, step, carried)

        def sem(name):
            return ctx.enter_context(nc.semaphore(name))

        NF = FF // P
        UN = 4
        NK = HB // P
        ident = sb("e_ident", [P, P])
        bias = sb("e_bias", [P, C])
        idx = sb("e_index", [P, NT, TOPK], I32)
        idxf = sb("e_idxf", [P, NT, TOPK])
        ew = sb("e_ew", [P, NT, TOPK])
        picked = sb("e_picked", [P, NE, NT, TOPK])
        gate = sb("e_gate", [P, NE, NT])
        x = sb("e_x", [P, NT, C])
        acc = sb("e_acc", [P, NT, C])
        xT = sb("e_xT", [P, CK, N_TOK])
        w1 = sb("e_w1", [P, 2, CK, FF])
        w2 = sb("e_w2", [P, 2, NF, C])
        hT = sb("e_hT", [P, 2, NF, HB])
        st = sb("e_st", [P, NT, 6])
        mv = sb("e_mv", [P, NT, 2])
        rs = sb("e_rs", [P, 3, NT])
        hid = [ctx.enter_context(nc.psum_tensor(f"e_h{i}", [P, HB], F32)) for i in range(4)]
        yp = [ctx.enter_context(nc.psum_tensor(f"e_y{i}", [P, HB], F32)) for i in range(4)]
        consts = sem("e_consts")
        gates, turned, xt_ready, acc_ready = sem("e_gates"), sem("e_turned"), sem("e_xt_ready"), sem("e_acc_ready")
        w1_here = [ev(f"e_w1_here{i}", 1, 16) for i in range(2)]
        w2_here = [ev(f"e_w2_here{i}", 1, 16) for i in range(2)]
        hidden = ev("e_hidden", UN * NF, carried=True)
        gelu = ev("e_gelu", UN * NF, carried=True)
        mixed = ev("e_mixed", UN * NK, carried=True)
        added = ev("e_added", UN * NK, carried=True)
        st_done, ln_chain, normed = sem("e_st_done"), sem("e_ln_chain"), sem("e_normed")
        var_ready, root_ready, out_sent = sem("e_var"), sem("e_root"), sem("e_out_sent")
        TURNS = NE // 2
        block = ctx.enter_context(nc.Block())

        @block.sync
        def _(sp):
            sp.dma_start(x[:], x_mid[0].rearrange("(n p) c -> p n c", p=P)).then_inc(consts, 16)
            for dst, name in ((ident, "ident"), (bias, "ffn_b"), (idx, "e_idx"), (ew, "e_w")):
                sp.dma_start(dst[:], io[name]).then_inc(consts, 16)
            with sp.Fori(0, TURNS) as b:
                for i in range(2):
                    sp.wait_ge(hidden.sem, hidden.before(b, (2 * i + 2) * NF - 1))
                    sp.dma_start(w1[:, i], io["w1"][bass.ds(b * 2 + i, 1)].rearrange("o (c p) f -> p (o c) f", p=P)) \
                        .then_inc(w1_here[i].sem, 16)
                    sp.wait_ge(mixed.sem, mixed.before(b, (2 * i + 2) * NK - 1))
                    sp.dma_start(w2[:, i], io["w2"][bass.ds(b * 2 + i, 1)].rearrange("o (f p) c -> p (o f) c", p=P)) \
                        .then_inc(w2_here[i].sem, 16)
            sp.wait_ge(normed, 1)
            sp.dma_start(io["out"][0].rearrange("(n p) c -> p n c", p=P), acc[:]).then_inc(out_sent, 16)
            sp.wait_ge(out_sent, 16)

        @block.tensor
        def _(pe):
            hidden.start(pe)
            mixed.start(pe)
            pe.wait_ge(consts, 16 * 5)
            for c in range(CK):
                for half in range(2):
                    bank = hid[2 * c + half]
                    for n in range(4):
                        m = pe.transpose(bank[:, n * P:(n + 1) * P], x[:, 4 * half + n, c * P:(c + 1) * P], ident[:])
                    m.then_inc(turned, 1)
            pe.wait_ge(xt_ready, 4)
            with pe.Fori(0, TURNS) as b:
                def first(u):
                    i, c = divmod(u, 2)
                    if c == 0:
                        pe.wait_ge(w1_here[i].sem, w1_here[i].at(b))
                    for f in range(NF):
                        y = u * NF + f
                        pe.wait_ge(gelu.sem, gelu.at(b, y - 4) if y >= 4 else gelu.before(b, UN * NF - 4 + y))
                        for k in range(CK):
                            m = pe.matmul(hid[y % 4][:], w1[:, i, k, f * P:(f + 1) * P], xT[:, k, HB * c:HB * c + HB],
                                          start=(k == 0), stop=(k == CK - 1))
                        m.then_inc(hidden.sem, 1)

                def second(u):
                    i, c = divmod(u, 2)
                    if c == 0:
                        pe.wait_ge(w2_here[i].sem, w2_here[i].at(b))
                    pe.wait_ge(gelu.sem, gelu.at(b, (u + 1) * NF - 1))
                    for n in range(NK):
                        y = u * NK + n
                        pe.wait_ge(added.sem, added.at(b, y - 4) if y >= 4 else added.before(b, UN * NK - 4 + y))
                        for f in range(NF):
                            m = pe.matmul(yp[y % 4][:, 0:C], hT[:, u % 2, f, n * P:(n + 1) * P], w2[:, i, f, :],
                                          start=(f == 0), stop=(f == NF - 1))
                        m.then_inc(mixed.sem, 1)

                for u in range(UN + 1):
                    if u < UN:
                        first(u)
                    if u:
                        second(u - 1)

        @block.scalar
        def _(act):
            gelu.start(act)
            for c in range(CK):
                for half in range(2):
                    act.wait_ge(turned, 2 * c + half + 1)
                    act.activation(xT[:, c, HB * half:HB * half + HB], hid[2 * c + half][:], ACT.Copy).then_inc(xt_ready, 1)
            with act.Fori(0, TURNS) as b:
                for u in range(UN):
                    act.wait_ge(mixed.sem, mixed.at(b, (u - 1) * NK - 1) if u >= 2 else
                                mixed.before(b, (UN + u - 1) * NK - 1))
                    for f in range(NF):
                        y = u * NF + f
                        act.wait_ge(hidden.sem, hidden.at(b, y))
                        act.activation(hT[:, u % 2, f, :], hid[y % 4][:], ACT.Gelu).then_inc(gelu.sem, 1)
            act.preload_act_table_set("natural_log_exp_and_others")
            act.wait_ge(var_ready, 1)
            act.activation(rs[:, 1], rs[:, 0], ACT.Ln).then_inc(root_ready, 1)
            act.wait_ge(root_ready, 1)
            act.activation(rs[:, 1], rs[:, 1], ACT.Exp, scale=-0.5).then_inc(root_ready, 1)

        @block.vector
        def _(dve):
            added.start(dve)
            dve.wait_ge(consts, 16 * 5)
            dve.tensor_copy(idxf[:], idx[:]).then_inc(gates, 1)
            dve.wait_ge(gates, 1)
            for e in range(NE):
                dve.scalar_tensor_tensor(picked[:, e], idxf[:], float(e), ew[:], ALU.is_equal, ALU.mult).then_inc(gates, 1)
            dve.wait_ge(gates, 1 + NE)
            dve.tensor_tensor(gate[:], picked[:, :, :, 0], picked[:, :, :, 1], ALU.add).then_inc(gates, 1)
            dve.tensor_tensor(acc[:], x[:], bias[:].unsqueeze(1).to_broadcast([P, NT, C]), ALU.add).then_inc(acc_ready, 1)
            dve.wait_ge(acc_ready, 1)
            dve.wait_ge(gates, 2 + NE)
            with dve.Fori(0, TURNS) as b:
                for u in range(UN):
                    i, c = divmod(u, 2)
                    for n in range(NK):
                        y, tile = u * NK + n, NK * c + n
                        dve.wait_ge(mixed.sem, mixed.at(b, y))
                        dve.wait_ge(added.sem, added.at(b, y - 2 * NK) if y >= 2 * NK else
                                    added.before(b, (UN - 2) * NK + y))
                        dve.scalar_tensor_tensor(acc[:, tile, :], yp[y % 4][:, 0:C],
                                                 gate[:, bass.ds(b * 2 + i, 1), tile], acc[:, tile, :],
                                                 ALU.mult, ALU.add).then_inc(added.sem, 1)
            dve.wait_ge(added.sem, added.at(TURNS - 1, UN * NK - 1))
            for n in range(NT):
                dve.bn_stats(st[:, n, :], acc[:, n, :]).then_inc(st_done, 1)
            for n in range(NT):
                dve.wait_ge(st_done, n + 1)
                dve.bn_aggr(mv[:, n, :], st[:, n, :]).then_inc(st_done, 1)
            dve.wait_ge(st_done, 2 * NT)
            dve.tensor_scalar(rs[:, 0], mv[:, :, 1], 1e-5, None, ALU.add).then_inc(var_ready, 1)
            dve.wait_ge(root_ready, 2)

            def step(k, ins):
                ins.then_inc(ln_chain, 1)
                dve.wait_ge(ln_chain, k)

            step(1, dve.tensor_tensor(rs[:, 2], rs[:, 0], rs[:, 1], ALU.mult))
            step(2, dve.tensor_tensor(rs[:, 2], rs[:, 2], rs[:, 1], ALU.mult))
            step(3, dve.tensor_scalar(rs[:, 2], rs[:, 2], -0.5, 1.5, ALU.mult, ALU.add))
            step(4, dve.tensor_tensor(rs[:, 1], rs[:, 1], rs[:, 2], ALU.mult))
            for n in range(NT):
                ins = dve.tensor_scalar(acc[:, n, :], acc[:, n, :], mv[:, n, 0:1], rs[:, 1, n:n + 1],
                                        ALU.subtract, ALU.mult)
            ins.then_inc(normed, 1)


def shape_constants():
    d = np.arange(P) % HD
    pos = np.arange(T, dtype=np.float32)
    inv = (np.float32(1.0) / np.float32(10000.0) ** (np.arange(0, HD, 2, dtype=np.float32) / np.float32(HD))).astype(np.float32)
    ang = (pos[None, :] * inv[d % (HD // 2)][:, None]).astype(np.float32)
    tabs = np.stack([np.cos(ang), np.where(d < HD // 2, 1.0, -1.0)[:, None] * np.sin(ang)], 1).astype(np.float32)
    rowind = np.zeros((P, 4, 16), np.float32)
    for g, first in enumerate((GW, 0, 0, GW)):
        for j in range(GW):
            h = first + j
            row = None
            if HYP0 <= h < COS0:
                row = h - HYP0 + (N_HYP if g >= 2 else 0)
            elif h >= COS0 and g >= 2:
                row = 2 * N_HYP + h - COS0
            if row is not None:
                rowind[j * HD:(j + 1) * HD, g, row] = 1.0
    cos_rows = (np.arange(P) // HD + GW) >= COS0
    blk = (np.arange(P)[:, None] // HD == np.arange(P)[None, :] // HD) & cos_rows[None, :]
    v_pad = np.zeros((P, 4, NT, 4, VW), np.float32)
    v_pad[..., HD] = 1.0
    first, second = np.arange(P)[:, None], np.arange(P)[None, :]
    masks = np.stack([second >= first, np.where(second < first, -1e25, 0.0), np.where(second > first, -1e25, 0.0),
                      np.where(second > first, 1e9, 0.0)], 1).astype(np.float32)
    return {
        "masks": masks,
        "ident": np.eye(P, dtype=np.float32),
        "tabs": tabs,
        "rowind": rowind,
        "blk": blk.astype(np.float32),
        "nhyp": (~cos_rows).astype(np.float32)[:, None],
        "v_pad": v_pad,
    }


def lay_out(L0_attn_x, L0_attn_qkv_w, L0_attn_curvature, L0_attn_proj_w, L0_attn_proj_b, L0_ffn_bias,
            L0_ffn_w1, L0_ffn_w2, L0_ffn_expert_indices, L0_ffn_expert_weights, L0_ffn_scores):
    w = np.asarray(L0_attn_qkv_w)
    swap = np.arange(2 * C).reshape(-1, 2, HD // 2)[:, ::-1].reshape(-1)
    packed = np.concatenate([np.arange(h * HD, h * HD + HD) for h in PACKED])
    w_all = np.concatenate([w[:2 * C], w[:2 * C][swap], w[2 * C:][packed]], 0)
    curv = np.asarray(L0_attn_curvature).reshape(-1)
    kcurv = np.zeros((P, 2, 2), np.float32)
    rcurv = np.zeros((16, 3), np.float32)
    rcurv[:, 0] = 1.0
    rcurv[0:N_HYP, 1] = 1.0
    rcurv[N_HYP:2 * N_HYP, 2] = 1.0
    kcurv[:, :, 1] = 1.0
    for i in range(N_HYP):
        g, row = (HYP0 + i) // GW, (HYP0 + i) % GW * HD
        kcurv[row:row + HD, g, 0] = curv[i]
        kcurv[row:row + HD, g, 1] = 0.0
        rcurv[[i, N_HYP + i], 0] = curv[i]
    return {
        "x": np.ascontiguousarray(L0_attn_x),
        "w_qkv": np.ascontiguousarray(w_all.T.reshape(CK, P, -1).transpose(1, 0, 2)),
        "acurv": np.ascontiguousarray(np.broadcast_to(curv, (P, N_HYP))),
        "w_proj": np.ascontiguousarray(np.asarray(L0_attn_proj_w).T[packed].reshape(CK, P, C).transpose(1, 0, 2)),
        "proj_b": np.asarray(L0_attn_proj_b)[None, :],
        "ffn_b": np.ascontiguousarray(np.broadcast_to(np.asarray(L0_ffn_bias), (P, C))),
        "w1": np.ascontiguousarray(L0_ffn_w1),
        "w2": np.ascontiguousarray(L0_ffn_w2),
        "e_idx": np.ascontiguousarray(np.asarray(L0_ffn_expert_indices).reshape(NT, P, TOPK).transpose(1, 0, 2)),
        "e_w": np.ascontiguousarray(np.asarray(L0_ffn_expert_weights).reshape(NT, P, TOPK).transpose(1, 0, 2)),
        "kcurv": kcurv,
        "rcurv": rcurv,
    }


def build(nc, io):
    def scratch(name, shape, dt=F32):
        return nc.dram_tensor(name, shape, dt, kind="Internal").ap()

    qk_parts = scratch("qk_parts", [B, 2, 3, C, T], BF16)
    t_parts = scratch("t_parts", [B, 2 * N_HYP, 3, T], BF16)
    v_rows = scratch("v_rows", [B, P, 4 * NT * 4 * VW])
    rk_cols = scratch("rk_cols", [B, P, NT * N_COS])
    m_parts = scratch("m_parts", [N_DOT * NT, 3, P], BF16)
    x_mid = scratch("x_mid", [B, T, C])
    project(nc, io, qk_parts, t_parts, v_rows, rk_cols)
    attend(nc, io, qk_parts, t_parts, v_rows, rk_cols, m_parts, x_mid)
    experts(nc, io, x_mid)


def kernel(**inputs):
    import concourse.bacc as bacc
    from concourse.bass_utils import run_bass_kernel_spmd

    nc = bacc.Bacc("TRN2", target_bir_lowering=False, num_devices=1)
    arrays = {f"in_{n}": np.asarray(a) for n, a in {**shape_constants(), **lay_out(**inputs)}.items()}
    io = {n[3:]: nc.dram_tensor(n, a.shape, mybir.dt.from_np(a.dtype), kind="ExternalInput").ap()
          for n, a in arrays.items()}
    io["out"] = nc.dram_tensor("out", (B, T, C), F32, kind="ExternalOutput").ap()
    build(nc, io)
    return run_bass_kernel_spmd(nc, [arrays], core_ids=[0]).results[0]["out"]
```

```python
from contextlib import ExitStack

import numpy as np
import concourse.bass as bass
from concourse import mybir

F32 = mybir.dt.float32
BF16 = mybir.dt.bfloat16
I32 = mybir.dt.int32
ALU = mybir.AluOpType
ACT = mybir.ActivationFunctionType
AX = mybir.AxisListType

P = 128
B, T, C = 8, 1024, 256
H, HD = 16, 16
N_DOT, N_HYP = 6, 4
N_COS = H - N_DOT - N_HYP
HYP0, COS0 = N_DOT, N_DOT + N_HYP
NT = T // P
CK = C // P
HB = 512
GW = P // HD
QPART = (0, 0, 1, 0, 2, 1)
KPART = (0, 1, 0, 2, 0, 1)
NPAIR = len(QPART)
KR = NPAIR * HD
NE, TOPK, FF = 8, 2, 1024
N_TOK = 1024
TINY = 1e-24
HYP_GROUP = tuple(range(HYP0, COS0))
GROUPS = ((12, 13, 14, 15), (10, 11, 4, 5), (0, 1, 2, 3), HYP_GROUP)
PACKED = tuple(h for g in GROUPS for h in g)
VW = 32


class Event:

    def __init__(self, ctx, nc, name, per=1, step=1, carried=False):
        self.sem = ctx.enter_context(nc.semaphore(name))
        self.per, self.step, self.carried = per, step, carried

    def start(self, engine):
        assert self.carried
        engine.sem_inc(self.sem, self.per * self.step)

    def at(self, turn, k=0):
        return turn * (self.per * self.step) + (k + 1 + self.per * self.carried) * self.step

    def before(self, turn, k=0):
        assert self.carried
        return turn * (self.per * self.step) + (k + 1) * self.step


def hold(engine, semaphore, value, passed):
    engine.wait_ge(semaphore, value)
    engine.sem_inc(passed, 1)


def project(nc, io, qk_parts, t_parts, v_rows, rk_cols):
    with ExitStack() as ctx:
        def sb(name, shape, dt=F32):
            return ctx.enter_context(nc.sbuf_tensor(name, shape, dt))

        def ev(name, per=1, step=1, carried=False):
            return Event(ctx, nc, name, per, step, carried)

        G = 4
        W_COL = (1, 0, 2, 3)
        SPLIT = (1, 0, 2, 3)
        ident = sb("p_ident", [P, P])
        w = sb("p_w", [P, CK, 5 * C])
        tabs = sb("p_tabs", [P, 2, T])
        ktabs = sb("p_ktabs", [P, 2, 2, T])
        kcurv = sb("p_kcurv", [P, 2, 2])
        kfac = sb("p_kfac", [P, 2])
        rcurv = sb("p_rcurv", [16, 3])
        radd = sb("p_radd", [16, 3])
        rowind = sb("p_rowind", [P, G, 16])
        blk = sb("p_blk", [P, P])
        nhyp = sb("p_nhyp", [P, 1])
        xin = sb("p_xin", [P, NT, C])
        xT = sb("p_xT", [P, CK, T])
        prod = sb("p_prod", [P, 2, T])
        rot = sb("p_rot", [P, G, T])
        sq = sb("p_sq", [P, G, T])
        fac = sb("p_fac", [P, T])
        parts = sb("p_parts", [P, 2, 3, T], BF16)
        rest = sb("p_rest", [P, T])
        vt = sb("p_vt", [P, 4, NT, 4, VW])
        ra = sb("p_ra", [16, T])
        rr = sb("p_rr", [16, T])
        rt = sb("p_rt", [16, T])
        tp = sb("p_tp", [16, 3, T], BF16)
        rk = sb("p_rk", [P, NT, N_COS])
        slot = [ctx.enter_context(nc.psum_tensor(f"p_ps{i}", [P, 2 * HB], F32)) for i in range(4)]

        consts = ctx.enter_context(nc.semaphore("p_consts"))
        NCONST = 9
        setup_dve = ctx.enter_context(nc.semaphore("p_setup_dve"))
        pe_passed = ctx.enter_context(nc.semaphore("p_pe_passed"))
        x_here = ev("p_x_here", 1, 16)
        x_turned = ev("p_x_turned", 2, carried=True)
        xt_ready = ev("p_xt_ready", 2)
        qk_ready = ev("p_qk_ready", 2 * G)
        v_ready = ev("p_v_ready", 2, carried=True)
        mul_done = ev("p_mul_done", 2 * G)
        rot_ready = ev("p_rot_ready", G, carried=True)
        sq_ready = ev("p_sq_ready", G)
        norm_ready, fac_max, fac_ln, fac_exp = ev("p_norm"), ev("p_fac_max"), ev("p_fac_ln"), ev("p_fac_exp")
        q_scaled = ev("p_q_scaled")
        hi_ready, rest_ready, mid_ready = ev("p_hi", G), ev("p_rest_r", G), ev("p_mid", G)
        lo_ready = ev("p_lo", G, carried=True)
        parts_sent = [ev(f"p_parts_sent{k}", 2, 16, carried=True) for k in range(2)]
        v_copied = ev("p_v_copied", 2)
        v_sent = ev("p_v_sent", 1, 16, carried=True)
        rows_ready = ev("p_rows", carried=True)
        ra_ready, r_ln, r_exp = ev("p_ra_r"), ev("p_r_ln"), ev("p_r_exp")
        r_step = ev("p_r_step", 9, carried=True)
        cols_ready, rk_ready = ev("p_cols", carried=True), ev("p_rk_r", carried=True)
        tp_sent, rk_sent = ev("p_tp_sent", 1, 16, carried=True), ev("p_rk_sent", 1, 16, carried=True)
        block = ctx.enter_context(nc.Block())

        @block.sync
        def _(sp):
            for dst, name in ((ident, "ident"), (w, "w_qkv"), (tabs, "tabs"), (kcurv, "kcurv"), (rcurv, "rcurv"),
                              (rowind, "rowind"), (blk, "blk"), (nhyp, "nhyp")):
                sp.dma_start(dst[:], io[name]).then_inc(consts, 16)
            sp.dma_start(vt[:], io["v_pad"]).then_inc(consts, 16)
            for k in range(2):
                parts_sent[k].start(sp)
            v_sent.start(sp)
            tp_sent.start(sp)
            rk_sent.start(sp)

            def store_parts(b, k):
                g = SPLIT[k]
                sp.wait_ge(lo_ready.sem, lo_ready.at(b, k))
                half = P if g in (0, 3) else 0
                sp.dma_start(qk_parts[bass.ds(b, 1), g // 2, :, half:half + P, :]
                             .rearrange("o s p t -> p (o s) t"), parts[:, k % 2]) \
                    .then_inc(parts_sent[k % 2].sem, 16)

            def store_rest(b):
                sp.wait_ge(v_copied.sem, v_copied.at(b, 1))
                sp.dma_start(v_rows[bass.ds(b, 1)].rearrange("o p f -> (o p) f"),
                             vt[:].rearrange("p g n h w -> p (g n h w)")).then_inc(v_sent.sem, 16)
                sp.wait_ge(rk_ready.sem, rk_ready.at(b))
                sp.dma_start(rk_cols[bass.ds(b, 1)].rearrange("o p f -> (o p) f"),
                             rk[:].rearrange("p n h -> p (n h)")).then_inc(rk_sent.sem, 16)
                sp.wait_ge(r_step.sem, r_step.at(b, 8))
                sp.dma_start(t_parts[bass.ds(b, 1)].rearrange("o r s t -> (o r) s t"), tp[0:2 * N_HYP]) \
                    .then_inc(tp_sent.sem, 16)

            def load_x(b):
                sp.wait_ge(x_turned.sem, x_turned.before(b, 1))
                sp.dma_start(xin[:], io["x"][bass.ds(b, 1)].rearrange("o (n p) c -> p (o n) c", p=P)) \
                    .then_inc(x_here.sem, 16)

            load_x(0)
            with sp.Fori(1, B) as b:
                load_x(b)
                for k in range(G):
                    store_parts(b - 1, k)
                store_rest(b - 1)
            for k in range(G):
                store_parts(B - 1, k)
            store_rest(B - 1)
            for k in range(2):
                sp.wait_ge(parts_sent[k].sem, parts_sent[k].at(B - 1, 1))
            sp.wait_ge(v_sent.sem, v_sent.at(B - 1))
            sp.wait_ge(tp_sent.sem, tp_sent.at(B - 1))
            sp.wait_ge(rk_sent.sem, rk_sent.at(B - 1))

        @block.tensor
        def _(pe):
            x_turned.start(pe)
            v_ready.start(pe)
            rows_ready.start(pe)
            cols_ready.start(pe)
            pe.wait_ge(consts, 16 * NCONST)

            def turn(b, first=False):
                pe.wait_ge(x_here.sem, x_here.at(b))
                if not first:
                    pe.wait_ge(v_copied.sem, v_copied.at(b - 1, 1))

                def turn_x(c, ps):
                    for n in range(NT):
                        m = pe.transpose(ps[:, n * P:(n + 1) * P], xin[:, n, c * P:(c + 1) * P], ident[:])
                    m.then_inc(x_turned.sem, 1)

                def product(g, swapped, ps):
                    o = (2 * C if swapped else 0) + W_COL[g] * P
                    for c in range(CK):
                        for t in range(0, T, HB):
                            m = pe.matmul(ps[:, t:t + HB], w[:, c, o:o + P], xT[:, c, t:t + HB],
                                          start=(c == 0), stop=(c == CK - 1))
                    m.then_inc(qk_ready.sem, 1)

                def values(half, ps):
                    for n in range(4):
                        tok = (half * 4 + n) * P
                        for c in range(CK):
                            m = pe.matmul(ps[:, n * C:(n + 1) * C], xT[:, c, tok:tok + P], w[:, c, 4 * C:5 * C],
                                          start=(c == 0), stop=(c == CK - 1))
                    m.then_inc(v_ready.sem, 1)

                turn_x(0, slot[2])
                turn_x(1, slot[3])
                pe.wait_ge(xt_ready.sem, xt_ready.at(b, 1))
                product(0, False, slot[1])
                product(0, True, slot[2])
                if not first:
                    columns(b - 1)
                product(1, False, slot[3])
                pe.wait_ge(rk_ready.sem, rk_ready.before(b))
                product(1, True, slot[0])
                pe.wait_ge(mul_done.sem, mul_done.at(b, 0))
                pe.wait_ge(sq_ready.sem, sq_ready.at(b, 0))
                for t in range(0, T, HB):
                    m = pe.matmul(slot[1][:, t:t + HB], blk[:], sq[:, 0, t:t + HB], start=True, stop=True)
                m.then_inc(norm_ready.sem, 1)
                pe.wait_ge(mul_done.sem, mul_done.at(b, 1))
                product(2, False, slot[2])
                pe.wait_ge(mul_done.sem, mul_done.at(b, 2))
                product(2, True, slot[3])
                pe.wait_ge(mul_done.sem, mul_done.at(b, 3))
                product(3, False, slot[0])
                pe.wait_ge(fac_max.sem, fac_max.at(b))
                product(3, True, slot[1])
                pe.wait_ge(mul_done.sem, mul_done.at(b, 4))
                values(0, slot[2])
                pe.wait_ge(mul_done.sem, mul_done.at(b, 5))
                values(1, slot[3])
                pe.wait_ge(mul_done.sem, mul_done.at(b, 6))
                pe.wait_ge(sq_ready.sem, sq_ready.at(b, G - 1))
                for t in range(0, T, HB):
                    for g in range(G):
                        m = pe.matmul(slot[0][0:16, t:t + HB], rowind[:, g, :], sq[:, g, t:t + HB],
                                      start=(g == 0), stop=(g == G - 1))
                m.then_inc(rows_ready.sem, 1)

            def columns(d):
                hold(pe, r_step.sem, r_step.at(d, 3), pe_passed)
                for n in range(NT):
                    m = pe.transpose(slot[0][:, n * 16:(n + 1) * 16], rr[:, n * P:(n + 1) * P], ident[0:16, 0:16])
                m.then_inc(cols_ready.sem, 1)

            turn(0, first=True)
            with pe.Fori(1, B) as b:
                turn(b)
            columns(B - 1)

        @block.scalar
        def _(act):
            act.preload_act_table_set("natural_log_exp_and_others")
            rk_ready.start(act)
            act.wait_ge(consts, 16 * NCONST)

            def roots(d):
                act.wait_ge(ra_ready.sem, ra_ready.at(d))
                act.wait_ge(cols_ready.sem, cols_ready.before(d))
                act.activation(rr[:], ra[:], ACT.Ln).then_inc(r_ln.sem, 1)
                act.wait_ge(r_ln.sem, r_ln.at(d))
                act.activation(rr[:], rr[:], ACT.Exp, scale=-0.5).then_inc(r_exp.sem, 1)

            def inverse_norms(d):
                act.wait_ge(cols_ready.sem, cols_ready.at(d))
                act.wait_ge(rk_sent.sem, rk_sent.before(d))
                act.activation(rk[:], slot[0][:, 0:NT * 16].rearrange("p (n r) -> p n r", r=16)
                               [:, :, 2 * N_HYP:2 * N_HYP + N_COS], ACT.Copy, scale=float(HD) ** 0.5) \
                    .then_inc(rk_ready.sem, 1)

            def square(b, g):
                act.wait_ge(rot_ready.sem, rot_ready.at(b, g))
                act.activation(sq[:, g, :], rot[:, g, :], ACT.Square).then_inc(sq_ready.sem, 1)

            def high_and_middle(b, k):
                g, sent = SPLIT[k], parts_sent[k % 2]
                if g == 0:
                    act.wait_ge(q_scaled.sem, q_scaled.at(b))
                act.wait_ge(sent.sem, sent.before(b, 1) if k < 2 else sent.at(b, 0))
                act.activation(parts[:, k % 2, 0, :], rot[:, g, :], ACT.Copy).then_inc(hi_ready.sem, 1)
                act.wait_ge(rest_ready.sem, rest_ready.at(b, k))
                act.activation(parts[:, k % 2, 1, :], rest[:], ACT.Copy).then_inc(mid_ready.sem, 1)

            def turn(b, first=False):
                act.wait_ge(v_ready.sem, v_ready.before(b, 1))
                for c in range(CK):
                    act.wait_ge(x_turned.sem, x_turned.at(b, c))
                    act.activation(xT[:, c, :], slot[2 + c][:], ACT.Copy).then_inc(xt_ready.sem, 1)
                if not first:
                    roots(b - 1)
                act.wait_ge(rows_ready.sem, rows_ready.before(b))
                square(b, 0)
                if not first:
                    inverse_norms(b - 1)
                square(b, 1)
                high_and_middle(b, 0)
                act.wait_ge(fac_max.sem, fac_max.at(b))
                act.activation(fac[:], fac[:], ACT.Ln).then_inc(fac_ln.sem, 1)
                act.wait_ge(fac_ln.sem, fac_ln.at(b))
                act.activation(fac[:], fac[:], ACT.Exp, scale=-0.5).then_inc(fac_exp.sem, 1)
                square(b, 2)
                high_and_middle(b, 1)
                square(b, 3)
                high_and_middle(b, 2)
                high_and_middle(b, 3)

            turn(0, first=True)
            with act.Fori(1, B) as b:
                turn(b)
            roots(B - 1)
            inverse_norms(B - 1)

        @block.vector
        def _(dve):
            lo_ready.start(dve)
            r_step.start(dve)
            rot_ready.start(dve)
            dve.wait_ge(consts, 16 * NCONST)
            dve.tensor_tensor(kfac[:], kcurv[:, :, 1], kcurv[:, :, 0], ALU.subtract).then_inc(setup_dve, 1)
            dve.reciprocal(radd[:, 0:1], rcurv[:, 0:1]).then_inc(setup_dve, 1)
            dve.wait_ge(setup_dve, 2)
            dve.tensor_tensor(radd[:, 1:2], radd[:, 0:1], rcurv[:, 1:2], ALU.mult).then_inc(setup_dve, 1)
            dve.tensor_tensor(radd[:, 2:3], rcurv[:, 0:1], rcurv[:, 2:3], ALU.mult).then_inc(setup_dve, 1)
            for i in range(2):
                dve.tensor_scalar(ktabs[:, i], tabs[:], kfac[:, i:i + 1], None, ALU.mult).then_inc(setup_dve, 1)
            dve.wait_ge(setup_dve, 6)
            dve.tensor_tensor(radd[:, 0:1], radd[:, 1:2], radd[:, 2:3], ALU.add).then_inc(setup_dve, 1)
            dve.wait_ge(setup_dve, 7)

            def turn(b, first=False):
                def rotate(g):
                    tab = tabs if g < 2 else ktabs[:, g - 2]
                    ps = (slot[1], slot[2], slot[3], slot[0], slot[2], slot[3], slot[0], slot[1])
                    dve.wait_ge(rot_ready.sem, rot_ready.at(b, g - 1) if g else rot_ready.before(b, G - 1))
                    for i in range(2):
                        dve.wait_ge(qk_ready.sem, qk_ready.at(b, 2 * g + i))
                        dve.tensor_tensor(prod[:, i, :], ps[2 * g + i][:], tab[:, i, :], ALU.mult) \
                            .then_inc(mul_done.sem, 1)
                    dve.wait_ge(mul_done.sem, mul_done.at(b, 2 * g + 1))
                    if g > 0:
                        dve.wait_ge(lo_ready.sem, lo_ready.before(b, SPLIT.index(g)))
                    dve.tensor_tensor(rot[:, g, :], prod[:, 0, :], prod[:, 1, :], ALU.add) \
                        .then_inc(rot_ready.sem, 1)

                def cut(k):
                    g = SPLIT[k]
                    buf = parts[:, k % 2]
                    dve.wait_ge(hi_ready.sem, hi_ready.at(b, k))
                    dve.tensor_tensor(rest[:], rot[:, g, :], buf[:, 0, :], ALU.subtract).then_inc(rest_ready.sem, 1)
                    dve.wait_ge(mid_ready.sem, mid_ready.at(b, k))
                    dve.tensor_tensor(buf[:, 2, :], rest[:], buf[:, 1, :], ALU.subtract).then_inc(lo_ready.sem, 1)
                    dve.wait_ge(lo_ready.sem, lo_ready.at(b, k))

                if not first:
                    clamp_rows(b - 1)
                    inverse_roots(b - 1)
                rotate(0)
                rotate(1)
                cut(0)
                if not first:
                    cut_roots(b - 1)
                dve.wait_ge(norm_ready.sem, norm_ready.at(b))
                dve.tensor_scalar(fac[:], slot[1][:], TINY, nhyp[:, 0:1], ALU.max, ALU.add).then_inc(fac_max.sem, 1)
                rotate(2)
                dve.wait_ge(fac_exp.sem, fac_exp.at(b))
                dve.wait_ge(sq_ready.sem, sq_ready.at(b, 0))
                dve.wait_ge(rot_ready.sem, rot_ready.at(b, 0))
                dve.tensor_tensor(rot[:, 0, :], rot[:, 0, :], fac[:], ALU.mult).then_inc(q_scaled.sem, 1)
                dve.wait_ge(q_scaled.sem, q_scaled.at(b))
                cut(1)
                rotate(3)
                cut(2)
                for half in range(2):
                    dve.wait_ge(v_ready.sem, v_ready.at(b, half))
                    dve.wait_ge(v_sent.sem, v_sent.before(b))
                    ps = slot[2 + half]
                    for grp in range(4):
                        ins = dve.tensor_copy(
                            vt[:, grp, half * 4:half * 4 + 4, :, 0:HD],
                            ps[:].rearrange("p (n g h d) -> p g n h d", n=4, g=4, h=4)[:, grp])
                    ins.then_inc(v_copied.sem, 1)
                cut(3)

            def clamp_rows(d):
                dve.wait_ge(rows_ready.sem, rows_ready.at(d))
                dve.tensor_scalar(ra[:], slot[0][0:16, :], radd[:, 0:1], TINY, ALU.add, ALU.max) \
                    .then_inc(ra_ready.sem, 1)

            def step(d, k, ins):
                ins.then_inc(r_step.sem, 1)
                dve.wait_ge(r_step.sem, r_step.at(d, k))

            def inverse_roots(d):
                dve.wait_ge(r_exp.sem, r_exp.at(d))
                step(d, 0, dve.tensor_tensor(rt[:], ra[:], rr[:], ALU.mult))
                step(d, 1, dve.tensor_tensor(rt[:], rt[:], rr[:], ALU.mult))
                step(d, 2, dve.tensor_scalar(rt[:], rt[:], -0.5, 1.5, ALU.mult, ALU.add))
                step(d, 3, dve.tensor_tensor(rr[:], rr[:], rt[:], ALU.mult))

            def cut_roots(d):
                step(d, 4, dve.tensor_tensor(rt[:], ra[:], rr[:], ALU.mult))
                dve.wait_ge(tp_sent.sem, tp_sent.before(d))
                step(d, 5, dve.tensor_copy(tp[:, 0, :], rt[:]))
                step(d, 6, dve.tensor_tensor(ra[:], rt[:], tp[:, 0, :], ALU.subtract))
                step(d, 7, dve.tensor_copy(tp[:, 1, :], ra[:]))
                step(d, 8, dve.tensor_tensor(tp[:, 2, :], ra[:], tp[:, 1, :], ALU.subtract))

            turn(0, first=True)
            with dve.Fori(1, B) as b:
                turn(b)
            clamp_rows(B - 1)
            inverse_roots(B - 1)
            cut_roots(B - 1)


def attend(nc, io, qk_parts, t_parts, v_rows, rk_cols, m_parts, x_mid):
    with ExitStack() as ctx:
        def sb(name, shape, dt=F32):
            return ctx.enter_context(nc.sbuf_tensor(name, shape, dt))

        def ev(name, per=1, step=1, carried=False):
            return Event(ctx, nc, name, per, step, carried)

        def sem(name):
            return ctx.enter_context(nc.semaphore(name))

        def psum(name):
            return ctx.enter_context(nc.psum_tensor(name, [P, HB], F32))

        NQ, NSLOT = 36, 4

        def quad(u):
            g, v = divmod(u, 12)
            c, j = (0, v) if v < 4 else (1, v - 4)
            t0 = max(HB * c, P * j)
            return g, c, j, t0, HB * (c + 1) - t0

        def pieces(i):
            w = P * (i + 1)
            return [(s0, min(HB, w - s0)) for s0 in range(0, w, HB)]

        def rows_of(h):
            if h < N_DOT:
                return KR + 3
            return KR + NPAIR if h < COS0 else KR

        NPAIRS = 2 * NT
        ORDER = (1, 0, 3, 2, 5, 7, 6, 4)

        def pair(n):
            i, p = ORDER[n // 2], n % 2
            return i, (HYP0 + 2 * p, HYP0 + 2 * p + 1), P * (i + 1), pieces(i)

        blocks = {n: [(j, k) for j in range(pair(n)[0] + 1) for k in range(2)] for n in range(NPAIRS)}
        turns = {n: [b_[q:q + 4] for q in range(0, len(b_), 4)] for n, b_ in blocks.items()}
        work = [[[] for _ in range(NSLOT)] for _ in range(NQ + 1)]

        def spread(u, items):
            for i, item in enumerate(items):
                work[u][i * NSLOT // len(items)].append(item)

        VALUES = 2
        for u in range(1, NQ + 1):
            work[u][VALUES if u < NQ else 0].append(("values", u - 1))
            if (u - 1) % 12 in (3, 11):
                work[u][VALUES + 1 if u < NQ else 0].append(("sums", 2 * ((u - 1) // 12) + ((u - 1) % 12 == 11)))
        for n in range(NPAIRS):
            spread(max(2 * n - 1, 0), [("argument", n, k, pc) for k in range(2) for pc in range(len(pair(n)[3]))])
            work[2 * n + 1][0].append(("log_square", n))
            work[2 * n + 1][2].append(("root", n))
            work[2 * n + 1][3].append(("add_root", n))
            work[2 * n + 2][0].append(("log_sum", n))
            work[2 * n + 2][1].append(("log_distance", n))
            work[2 * n + 2][2].append(("inverse", n))
            work[2 * n + 2][3].append(("row_bias", n))
            work[2 * n + 3][1].append(("hyp_exp", n, 0))
            work[2 * n + 3][3].append(("hyp_exp", n, 1))
            spread(2 * n + 4, [("turn", n, q) for q in range(len(turns[n]))])
            if n % 2:
                ends = [pair(n)[0] * k // NSLOT + 1 if k else 0 for k in range(NSLOT + 1)]
                for k in range(NSLOT):
                    if ends[k] < ends[k + 1]:
                        work[2 * n + 5][k].append(("hyp_values", n // 2, ends[k], ends[k + 1]))
                work[2 * n + 5][NSLOT - 1].append(("hyp_sums", n // 2))
        ROUNDS = (((4, 5), 1, 0, 7), ((0, 1, 2, 3), 2, 7, 13))
        MAXIMA = [[(h, i, pc, s0, w) for h in hs for i in range(NT) for pc, (s0, w) in enumerate(pieces(i))]
                  for hs, _, _, _ in ROUNDS]
        for r, (_, _, first_step, steps) in enumerate(ROUNDS):
            for u in range(steps):
                spread(first_step + u, [("maximum", r, m) for m in range(len(MAXIMA[r]))
                                        if m * steps // len(MAXIMA[r]) == u])
            work[first_step + steps][1].append(("join_maxima", r))
            work[first_step + steps][3].append(("turn_maxima", r))

        def columns_of(r):
            hs = ROUNDS[r][0]
            return hs[0] * NT, (hs[-1] + 1) * NT

        for n in range(NT):
            work[10 + 2 * n][1].append(("turn_rows", n))
            work[11 + 2 * n][1].append(("project", n))
            work[12 + 2 * n][2].append(("statistics", 0, n, n + 1))
            work[29 + n if n < NT // 2 else n - NT // 2][1].append(("turn_sums", n))
        work[27][0].append(("variance", 0))
        work[27][3].append(("inverse_root", 0))
        work[28][1].append(("normalize", 0))
        work[29][2].append(("add_bias",))
        work[30][1].append(("statistics", 1, 0, NT // 2))
        work[30][3].append(("statistics", 1, NT // 2, NT))
        work[31][1].append(("variance", 1))
        work[31][3].append(("inverse_root", 1))
        work[32][1].append(("normalize", 1))
        RINGED = ("argument", "maximum", "turn_maxima", "turn_rows", "project", "turn_sums", "turn")
        ringed = [item for step in work for slot in step for item in slot if item[0] in RINGED]
        WB = 3
        MORE = -len(ringed) % WB
        n_wide = len(ringed) + MORE
        m_item = ringed.index(("turn_maxima", 1))
        wide = {item: x + MORE * (x > m_item) for x, item in enumerate(ringed)}
        last_argument = [item for item in ringed if item[0] == "argument"][-1]
        LATE = ("turn_rows", "project", "statistics", "variance", "inverse_root", "normalize", "add_bias")

        def is_late(item):
            return item[0] in LATE or item[0] == "turn_sums" and item[1] >= NT // 2

        tail = [("turn_sums", n) for n in range(NT // 2, NT)] + [("turn_rows", 0)]
        for n in range(NT):
            tail += [("turn_rows", n + 1)] * (n + 1 < NT) + [("project", n), ("statistics", 0, n, n + 1)]
        tail += [("variance", 0), ("inverse_root", 0), ("normalize", 0), ("add_bias",), ("statistics", 1, 0, NT),
                 ("variance", 1), ("inverse_root", 1), ("normalize", 1)]
        tail_wide = {item: x for x, item in enumerate([it for it in tail if it[0] in RINGED])}
        RB = 3

        def last_turn(n):
            return wide["turn", n, len(turns[n]) - 1]

        def r_before(n):
            if n >= RB:
                return n - RB, False
            return max(m for m in range(NPAIRS) if m % RB == n % RB), True

        ident = sb("a_ident", [P, P])
        identb = sb("a_identb", [P, P], BF16)
        masks = sb("a_masks", [P, 4, P])
        masksb = sb("a_masksb", [P, 3, P], BF16)
        curv = sb("a_curv", [P, N_HYP])
        root = sb("a_root", [P, 4, N_HYP])
        wproj = sb("a_wproj", [P, CK, C])
        bias = sb("a_bias", [1, C])
        ones = sb("a_ones", [1, P])
        bias2 = sb("a_bias2", [P, C])
        Qb = sb("a_Q", [P, H, T], BF16)
        Kb = sb("a_K", [P, H, T], BF16)
        V = sb("a_V", [P, 4, NT, 4, VW])
        rk = sb("a_rk", [P, NT, N_COS])
        PT = sb("a_PT", [P, 2, 4, HB])
        mx = sb("a_mx", [P, 2, N_DOT * NT])
        M_ROWS = 4 * NT
        mrow = sb("a_mrow", [M_ROWS, 2, P])
        mpart = sb("a_mpart", [M_ROWS, 2, 3, P], BF16)
        ZW = T + 2
        Z = sb("a_Z", [P, 2, 2, ZW])
        R = sb("a_R", [P, RB, 2, ZW])
        nb = sb("a_nb", [P, 2, 2, 2])
        PTh = sb("a_PTh", [P, NT, 4, P])
        O = sb("a_O", [P, 4, T])
        X = sb("a_X", [P, NT, C])
        X3 = sb("a_X3", [P, NT, C])
        Y = sb("a_Y", [P, NT, H, HD])
        rden = sb("a_rden", [P, 2, H])
        YT = sb("a_YT", [P, 2, CK, P])
        st = sb("a_st", [P, NT, 6])
        mv = sb("a_mv", [P, NT, 2])
        rs = sb("a_rs", [P, 3, NT])
        sB = [psum(f"a_s{i}") for i in range(3)]
        oB = psum("a_o")
        wB = [psum(f"a_w{i}") for i in range(WB)]
        oH = psum("a_oh")

        consts, setup, act_setup = sem("a_consts"), sem("a_setup"), sem("a_act_setup")
        dve_passed, pool_passed, sp_passed = sem("a_dve_passed"), sem("a_pool_passed"), sem("a_sp_passed")
        NCONST = 7
        NLOAD = {0: 12, 1: 24, 2: 12, 3: 24}
        qk_here = {g: ev(f"a_qk_here{g}", 1, 16 * NLOAD[g]) for g in range(4)}
        m_sent = ev("a_m_sent", 2, 16)
        m_here = [ev(f"a_m_here{r}", 1, 16 * len(hs)) for r, (hs, _, _, _) in enumerate(ROUNDS)]
        v_here = {g: ev(f"a_v_here{g}", 1, 16) for g in range(4)}
        rk_here, x_here = ev("a_rk_here", 1, 16), ev("a_x_here", 1, 16)
        score = ev("a_score", NQ * 4, carried=True)
        prob = ev("a_prob", NQ * 4, carried=True)
        valued = ev("a_valued", NQ, carried=True)
        o_copied = ev("a_o_copied", 6, carried=True)
        wide_full, wide_free = ev("a_wide_full", n_wide, carried=True), ev("a_wide_free", n_wide, carried=True)
        m_step = ev("a_m_step", 12)
        z_sq = ev("a_z_sq", NPAIRS)
        z_ln, z_root = ev("a_z_ln", NPAIRS), ev("a_z_root", NPAIRS)
        z_sum = ev("a_z_sum", NPAIRS)
        d_ln, d_ln2 = ev("a_d_ln", NPAIRS), ev("a_d_ln2", 2 * NPAIRS)
        d_inv = ev("a_d_inv", NPAIRS, carried=True)
        b_max, b_ready = ev("a_b_max", NPAIRS), ev("a_b_ready", NPAIRS)
        h_prob = ev("a_h_prob", 2 * NPAIRS)
        h_valued, h_copied = ev("a_h_valued", NT, carried=True), ev("a_h_copied", NT, carried=True)
        y_inv, stats = ev("a_y_inv", NT), ev("a_stats", 4 * NT)
        var_ready, rs_ln, rs_exp = ev("a_var", 2), ev("a_rs_ln", 2), ev("a_rs_exp", 2)
        rs_step, normed = ev("a_rs_step", 8), ev("a_normed", 2)
        biased = ev("a_biased")
        mid_sent, out_sent = ev("a_mid_sent", 1, 16), ev("a_out_sent", 1, 16)
        x3_sent = ev("a_x3_sent", carried=True)
        block = ctx.enter_context(nc.Block())

        @block.sync
        def _(sp):
            for dst, name in ((ident, "ident"), (masks, "masks"), (curv, "acurv"), (wproj, "w_proj"),
                              (bias, "proj_b"), (bias2, "ffn_b")):
                sp.dma_start(dst[:], io[name]).then_inc(consts, 16)
            sp.dma_start(root[:, 0], io["acurv"]).then_inc(consts, 16)
            with sp.Fori(0, B) as b:
                def heads(g, runs):
                    for qk, buf, order in ((0, Qb, QPART), (1, Kb, KPART)):
                        for r, part in enumerate(order):
                            for h0, h1 in runs:
                                src = qk_parts[bass.ds(b, 1), qk, part, h0 * HD:h1 * HD, :]
                                sp.dma_start(buf[r * HD:(r + 1) * HD, h0:h1, :],
                                             src.rearrange("o (h d) t -> d (o h) t", d=HD)) \
                                    .then_inc(qk_here[g].sem, 16)

                def values(g):
                    sp.dma_start(V[:, g].rearrange("p n h w -> p (n h w)"),
                                 v_rows[bass.ds(b, 1), :, g * NT * 4 * VW:(g + 1) * NT * 4 * VW]
                                 .rearrange("o p f -> (o p) f")).then_inc(v_here[g].sem, 16)

                def inverse_norms():
                    sp.dma_start(rk[:].rearrange("p n h -> p (n h)"),
                                 rk_cols[bass.ds(b, 1)].rearrange("o p f -> (o p) f")).then_inc(rk_here.sem, 16)

                sp.wait_ge(valued.sem, valued.before(b, 11))
                heads(0, ((12, 16),))
                values(0)
                hold(sp, valued.sem, valued.before(b, 23), sp_passed)
                heads(1, ((4, 6), (10, 12)))
                values(1)
                hold(sp, wide_full.sem, wide_full.before(b, wide[last_argument]), sp_passed)
                heads(3, ((HYP0, COS0),))
                for i in range(NPAIR):
                    for buf, first, order in ((Qb, 0, QPART), (Kb, N_HYP, KPART)):
                        sp.dma_start(buf[KR + i:KR + i + 1, HYP0:COS0, :],
                                     t_parts[bass.ds(b, 1), first:first + N_HYP, order[i], :]) \
                            .then_inc(qk_here[3].sem, 16)
                sp.wait_ge(prob.sem, prob.before(b, 4 * 24 - 1))
                inverse_norms()
                hold(sp, valued.sem, valued.before(b, NQ - 1), sp_passed)
                heads(2, ((0, 4),))
                values(2)
                sp.wait_ge(h_valued.sem, h_valued.before(b, NT - 1))
                values(3)
                for r, (hs, _, _, _) in enumerate(ROUNDS):
                    c0, c1 = columns_of(r)
                    sp.wait_ge(m_step.sem, m_step.at(b, 6 * r + 5))
                    sp.dma_start(m_parts[c0:c1], mpart[0:c1 - c0, r]).then_inc(m_sent.sem, 16)
                    sp.wait_ge(m_sent.sem, m_sent.at(b, r))
                    for h in hs:
                        sp.dma_start(Qb[KR:KR + 3, h, :].rearrange("r (i c) -> r i c", c=P),
                                     m_parts[h * NT:(h + 1) * NT].rearrange("i r c -> r i c")) \
                            .then_inc(m_here[r].sem, 16)

        @block.tensor
        def _(pe):
            for e in (score, valued, wide_full, h_valued):
                e.start(pe)
            pe.wait_ge(consts, 16 * NCONST)
            pe.wait_ge(setup, 4)

            def scores(b, u, k):
                g, c, j, t0, w = quad(u)
                h, x = GROUPS[g][k], 4 * u + k
                pe.wait_ge(prob.sem, prob.at(b, x - 3) if x >= 3 else prob.before(b, 4 * NQ - 3 + x))
                bank, r = sB[x % 3], rows_of(h)
                diag = t0 == P * j
                m = pe.matmul(bank[:, 0:w], Kb[0:r, h, P * j:P * j + P], Qb[0:r, h, t0:t0 + w],
                              start=True, stop=not diag)
                if diag:
                    m = pe.matmul(bank[:, 0:P], identb[:], masksb[:, 0, :], start=False, stop=True)
                m.then_inc(score.sem, 1)

            def apply_values(b, u):
                g, c, j, t0, w = quad(u)
                pe.wait_ge(prob.sem, prob.at(b, 4 * u + 3))
                if j == 0:
                    n = 2 * g + c
                    pe.wait_ge(o_copied.sem, o_copied.at(b, n - 1) if n else o_copied.before(b, 5))
                    pe.wait_ge(v_here[g].sem, v_here[g].at(b))
                for k in range(4):
                    m = pe.matmul(oB[VW * k:VW * k + VW, t0 - HB * c:t0 - HB * c + w], V[:, g, j, k, :],
                                  PT[:, u % 2, k, 0:w], start=(j == 0), stop=(j == 4 * c + 3))
                m.then_inc(valued.sem, 1)

            def wide_bank(b, x):
                pe.wait_ge(wide_free.sem, wide_free.at(b, x - WB) if x >= WB else wide_free.before(b, n_wide - WB + x))
                return wB[x % WB]

            def row_scores(b, x, h, i, s0, w, mask):
                bank = wide_bank(b, x)
                diag = s0 + w == P * (i + 1)
                r = KR if h < N_DOT else rows_of(h)
                m = pe.matmul(bank[:, 0:w], Qb[0:r, h, P * i:P * i + P], Kb[0:r, h, s0:s0 + w],
                              start=True, stop=not diag)
                if diag:
                    m = pe.matmul(bank[:, w - P:w], identb[:], masksb[:, mask, :], start=False, stop=True)
                m.then_inc(wide_full.sem, 1)

            def turn_pair(b, n, q):
                if q == 0:
                    pe.wait_ge(h_prob.sem, h_prob.at(b, 2 * n + 1))
                bank = wide_bank(b, wide["turn", n, q])
                for a, (j, k) in enumerate(turns[n][q]):
                    m = pe.transpose(bank[:, a * P:(a + 1) * P], R[:, n % RB, k, P * j:P * j + P], ident[:])
                m.then_inc(wide_full.sem, 1)

            def apply_hyp_values(b, e, j0, j1):
                i, o = ORDER[e], P * (e % 4)
                if j0 == 0:
                    pe.wait_ge(wide_free.sem, wide_free.at(b, last_turn(2 * e + 1)))
                    pe.wait_ge(h_copied.sem, h_copied.at(b, e - 1) if e else h_copied.before(b, NT - 1))
                    if e == 0:
                        pe.wait_ge(v_here[3].sem, v_here[3].at(b))
                for j in range(j0, j1):
                    for k in range(4):
                        m = pe.matmul(oH[VW * k:VW * k + VW, o:o + P], V[:, 3, j, k, :], PTh[:, j, k, :],
                                      start=(j == 0), stop=(j == i))
                if j1 == i + 1:
                    m.then_inc(h_valued.sem, 1)

            def turn_sums(b, d, n, x):
                bank = wide_bank(b, x)
                pe.wait_ge(o_copied.sem, o_copied.at(d, 4 if n < NT // 2 else 5))
                pe.wait_ge(h_copied.sem, h_copied.at(d, ORDER.index(n)))
                for g in range(4):
                    m = pe.transpose(bank[:, g * P:(g + 1) * P], O[:, g, n * P:(n + 1) * P], ident[:])
                m.then_inc(wide_full.sem, 1)

            def turn_rows(b, n, x):
                bank = wide_bank(b, x)
                for c in range(CK):
                    m = pe.transpose(bank[:, c * P:(c + 1) * P],
                                     Y[:, n].rearrange("p h d -> p (h d)")[:, c * P:(c + 1) * P], ident[:])
                m.then_inc(wide_full.sem, 1)

            def project_rows(b, n, index):
                x, turned = index["project", n], index["turn_rows", n]
                if turned > x - WB:
                    pe.wait_ge(wide_free.sem, wide_free.at(b, turned))
                    bank = wB[x % WB]
                else:
                    bank = wide_bank(b, x)
                for c in range(CK):
                    pe.matmul(bank[:, 0:C], YT[:, n % 2, c, :], wproj[:, c, :], start=(c == 0), stop=False)
                pe.matmul(bank[:, 0:C], ones[:], bias[:], start=False, stop=True).then_inc(wide_full.sem, 1)

            def late(b, d, item, index):
                if item[0] == "turn_sums":
                    turn_sums(b, d, item[1], index[item])
                elif item[0] == "turn_rows":
                    turn_rows(b, item[1], index[item])
                else:
                    project_rows(b, item[1], index)

            def do(b, item):
                kind = item[0]
                if kind == "values":
                    apply_values(b, item[1])
                elif kind == "argument":
                    _, n, k, pc = item
                    i, hs, _, pcs = pair(n)
                    if n == 0 and k == 0:
                        pe.wait_ge(qk_here[3].sem, qk_here[3].at(b))
                    row_scores(b, wide[item], hs[k], i, *pcs[pc], 2)
                elif kind == "maximum":
                    h, i, pc, s0, w = MAXIMA[item[1]][item[2]]
                    if item[2] == 0:
                        g = ROUNDS[item[1]][1]
                        pe.wait_ge(qk_here[g].sem, qk_here[g].at(b))
                    row_scores(b, wide[item], h, i, s0, w, 1)
                elif kind == "turn_maxima":
                    bank = wide_bank(b, wide[item])
                    r = item[1]
                    c0, c1 = columns_of(r)
                    pe.wait_ge(m_step.sem, m_step.at(b, 6 * r + 1))
                    pe.transpose(bank[0:c1 - c0, 0:P], mx[:, 0, c0:c1], ident[:]).then_inc(wide_full.sem, 1 + MORE * r)
                elif kind == "turn":
                    turn_pair(b, item[1], item[2])
                elif kind == "hyp_values":
                    apply_hyp_values(b, *item[1:])
                elif kind == "turn_sums":
                    turn_sums(b, b, item[1], wide[item])

            def turn(b, first=False):
                for u, step in enumerate(work):
                    for k, slot in enumerate(step):
                        if u < NQ:
                            if k == 0 and u == 0:
                                pe.wait_ge(qk_here[0].sem, qk_here[0].at(b))
                            if k == 0 and u in (12, 24):
                                here = m_here[u // 24]
                                pe.wait_ge(here.sem, here.at(b))
                            scores(b, u, k)
                        for item in slot:
                            if is_late(item) and item[0] in RINGED:
                                if first:
                                    wide_bank(b, wide[item])
                                    pe.wait_ge(wide_full.sem, wide_full.at(b, wide[item] - 1))
                                    pe.sem_inc(wide_full.sem, 1)
                                else:
                                    late(b, b - 1, item, wide)
                            else:
                                do(b, item)

            turn(0, first=True)
            with pe.Fori(1, B) as b:
                turn(b)
            for item in tail:
                if item[0] in RINGED:
                    late(B, B - 1, item, tail_wide)

        @block.scalar
        def _(act):
            act.preload_act_table_set("natural_log_exp_and_others")
            prob.start(act)
            d_inv.start(act)
            act.wait_ge(consts, 16 * NCONST)
            act.activation(root[:, 0], curv[:], ACT.Ln).then_inc(act_setup, 1)
            act.wait_ge(act_setup, 1)
            act.activation(root[:, 0], root[:, 0], ACT.Exp, scale=0.5).then_inc(act_setup, 1)
            act.wait_ge(setup, 8)

            def exponentials(b, u, k):
                g, c, j, t0, w = quad(u)
                h, x = GROUPS[g][k], 4 * u + k
                act.wait_ge(valued.sem, valued.at(b, u - 2) if u >= 2 else valued.before(b, NQ - 2 + u))
                act.wait_ge(score.sem, score.at(b, x))
                scale = rk[:, j, h - COS0:h - COS0 + 1] if h >= COS0 else float(HD) ** -0.5
                act.activation(PT[:, u % 2, k, 0:w], sB[x % 3][:, 0:w], ACT.Exp, scale=scale).then_inc(prob.sem, 1)

            def do(b, item):
                kind, n = item[0], item[1] if len(item) > 1 else None
                if kind in ("log_square", "root", "log_sum", "log_distance", "inverse", "hyp_exp"):
                    _, hs, w, pcs = pair(n)
                    ww = w + len(pcs)
                    z, r = Z[:, n % 2, :, 0:ww], R[:, n % RB, :, 0:ww]
                if kind == "log_square":
                    act.wait_ge(z_sq.sem, z_sq.at(b, n))
                    act.activation(r, r, ACT.Ln, bias=-1.0).then_inc(z_ln.sem, 1)
                elif kind == "root":
                    act.wait_ge(z_ln.sem, z_ln.at(b, n))
                    act.activation(r, r, ACT.Exp, scale=0.5).then_inc(z_root.sem, 1)
                elif kind == "log_sum":
                    act.wait_ge(z_sum.sem, z_sum.at(b, n))
                    act.activation(r, z, ACT.Ln).then_inc(d_ln.sem, 1)
                elif kind == "log_distance":
                    act.wait_ge(d_ln.sem, d_ln.at(b, n))
                    for k, h in enumerate(hs):
                        act.activation(Z[:, n % 2, k, 0:ww], R[:, n % RB, k, 0:ww], ACT.Ln,
                                       bias=root[:, 3, h - HYP0:h - HYP0 + 1]).then_inc(d_ln2.sem, 1)
                elif kind == "inverse":
                    act.wait_ge(d_ln2.sem, d_ln2.at(b, 2 * n + 1))
                    act.activation(r, z, ACT.Exp, scale=-1.0).then_inc(d_inv.sem, 1)
                elif kind == "hyp_exp":
                    k = item[2]
                    if k == 0:
                        act.wait_ge(b_ready.sem, b_ready.at(b, n))
                    act.activation(R[:, n % RB, k, 0:w], R[:, n % RB, k, 0:w], ACT.Exp,
                                   scale=root[:, 0, hs[k] - HYP0:hs[k] - HYP0 + 1],
                                   bias=nb[:, n % 2, 1, k:k + 1]).then_inc(h_prob.sem, 1)

            def inverse_root(d, a):
                act.wait_ge(var_ready.sem, var_ready.at(d, a))
                act.activation(rs[:, 1], rs[:, 0], ACT.Ln).then_inc(rs_ln.sem, 1)
                act.wait_ge(rs_ln.sem, rs_ln.at(d, a))
                act.activation(rs[:, 1], rs[:, 1], ACT.Exp, scale=-0.5).then_inc(rs_exp.sem, 1)

            def turn(b, first=False):
                for u, step in enumerate(work):
                    for k, slot in enumerate(step):
                        if u < NQ:
                            if k == 0 and u == 0:
                                act.wait_ge(rk_here.sem, rk_here.at(b))
                            exponentials(b, u, k)
                        for item in slot:
                            if item[0] not in LATE:
                                do(b, item)
                            elif item[0] == "inverse_root" and not first:
                                inverse_root(b - 1, item[1])

            turn(0, first=True)
            with act.Fori(1, B) as b:
                turn(b)
            for a in range(2):
                inverse_root(B - 1, a)

        @block.gpsimd
        def _(pool):
            def squares(b):
                for n in range(NPAIRS):
                    _, _, w, pcs = pair(n)
                    ww = w + len(pcs)
                    pool.wait_ge(wide_free.sem, wide_free.at(b, wide["argument", n, 1, len(pcs) - 1]))
                    m, earlier = r_before(n)
                    pool.wait_ge(wide_full.sem, (wide_full.before if earlier else wide_full.at)(b, last_turn(m)))
                    pool.tensor_tensor(R[:, n % RB, :, 0:ww], Z[:, n % 2, :, 0:ww], Z[:, n % 2, :, 0:ww], ALU.mult) \
                        .then_inc(z_sq.sem, 1)

            def rows_out(d):
                for a, (dram, rows, sent) in enumerate(((x_mid, X, mid_sent), (io["out"], X3, out_sent))):
                    hold(pool, normed.sem, normed.at(d, a), pool_passed)
                    pool.dma_start(dram[bass.ds(d, 1)].rearrange("o (n p) c -> p (o n) c", p=P), rows[:]) \
                        .then_inc(sent.sem, 16)

            def rows_in(b):
                pool.dma_start(X[:], io["x"][bass.ds(b, 1)].rearrange("o (n p) c -> p (o n) c", p=P)) \
                    .then_inc(x_here.sem, 16)

            x3_sent.start(pool)
            squares(0)
            rows_in(0)
            with pool.Fori(1, B) as b:
                squares(b)
                rows_out(b - 1)
                hold(pool, mid_sent.sem, mid_sent.at(b - 1), pool_passed)
                rows_in(b)
                hold(pool, out_sent.sem, out_sent.at(b - 1), x3_sent.sem)
            rows_out(B - 1)
            pool.wait_ge(mid_sent.sem, mid_sent.at(B - 1))
            pool.wait_ge(out_sent.sem, out_sent.at(B - 1))

        @block.vector
        def _(dve):
            for e in (wide_free, o_copied, h_copied):
                e.start(dve)
            dve.memset(Kb[KR:KR + 3, 0:N_DOT, :], 1.0).then_inc(setup, 1)
            dve.memset(ones[:], 1.0).then_inc(setup, 1)
            dve.memset(mx[:], -3.0e38).then_inc(setup, 1)
            dve.wait_ge(consts, 16 * NCONST)
            dve.wait_ge(setup, 3)
            dve.tensor_copy(identb[:], ident[:])
            dve.tensor_copy(masksb[:], masks[:, 1:4, :]).then_inc(setup, 1)
            dve.wait_ge(act_setup, 2)
            dve.reciprocal(root[:, 1], root[:, 0]).then_inc(setup, 1)
            dve.wait_ge(setup, 5)
            dve.tensor_tensor(root[:, 1], root[:, 1], curv[:], ALU.mult).then_inc(setup, 1)
            dve.wait_ge(setup, 6)
            dve.tensor_tensor(root[:, 1], root[:, 1], root[:, 0], ALU.add).then_inc(setup, 1)
            dve.wait_ge(setup, 7)
            dve.tensor_scalar(root[:, 2], root[:, 1], -0.5, None, ALU.mult)
            dve.tensor_scalar(root[:, 3], root[:, 1], 0.5e-6, None, ALU.mult)
            dve.tensor_scalar(root[:, 0], root[:, 1], 0.5, None, ALU.mult).then_inc(setup, 1)
            dve.wait_ge(setup, 8)

            def clamp(b, n, k, pc):
                _, _, w, pcs = pair(n)
                s0, pw = pcs[pc]
                x = wide["argument", n, k, pc]
                if k == 0 and pc == 0:
                    dve.wait_ge(d_inv.sem, d_inv.at(b, n - 2) if n >= 2 else d_inv.before(b, NPAIRS - 2 + n))
                dve.wait_ge(wide_full.sem, wide_full.at(b, x))
                dve.tensor_scalar(Z[:, n % 2, k, s0:s0 + pw], wB[x % WB][:, 0:pw],
                                  float(np.float32(1.0 + 1e-7)), 3.0e38, ALU.max, ALU.min,
                                  accum_out=Z[:, n % 2, k, w + pc:w + pc + 1]).then_inc(wide_free.sem, 1)

            def row_maximum(b, r, m):
                h, i, pc, s0, w = MAXIMA[r][m]
                x, col = wide["maximum", r, m], h * NT + i
                dve.wait_ge(wide_full.sem, wide_full.at(b, x))
                dve.tensor_reduce(mx[:, pc, col:col + 1], wB[x % WB][:, 0:w], AX.X, ALU.max).then_inc(wide_free.sem, 1)

            def join_maxima(b, r):
                c0, c1 = columns_of(r)
                dve.wait_ge(wide_free.sem, wide_free.at(b, wide["maximum", r, len(MAXIMA[r]) - 1]))
                dve.tensor_tensor(mx[:, 0, c0:c1], mx[:, 0, c0:c1], mx[:, 1, c0:c1], ALU.max).then_inc(m_step.sem, 1)
                dve.wait_ge(m_step.sem, m_step.at(b, 6 * r))
                dve.tensor_scalar(mx[:, 0, c0:c1], mx[:, 0, c0:c1], -1.0, None, ALU.mult).then_inc(m_step.sem, 1)

            def cut_maxima(b, r):
                x, c0, c1 = wide["turn_maxima", r], *columns_of(r)
                row, rest, part = mrow[0:c1 - c0, 0, :], mrow[0:c1 - c0, 1, :], mpart[0:c1 - c0, r]
                dve.wait_ge(wide_full.sem, wide_full.at(b, x + MORE * r))
                if r:
                    dve.wait_ge(m_step.sem, m_step.at(b, 6 * r - 1))
                dve.tensor_copy(row, wB[x % WB][0:c1 - c0, 0:P]).then_inc(wide_free.sem, 1 + MORE * r)
                dve.wait_ge(wide_free.sem, wide_free.at(b, x + MORE * r))
                dve.tensor_copy(part[:, 0, :], row).then_inc(m_step.sem, 1)
                dve.wait_ge(m_step.sem, m_step.at(b, 6 * r + 2))
                dve.tensor_tensor(rest, row, part[:, 0, :], ALU.subtract).then_inc(m_step.sem, 1)
                dve.wait_ge(m_step.sem, m_step.at(b, 6 * r + 3))
                dve.tensor_copy(part[:, 1, :], rest).then_inc(m_step.sem, 1)
                dve.wait_ge(m_step.sem, m_step.at(b, 6 * r + 4))
                dve.tensor_tensor(part[:, 2, :], rest, part[:, 1, :], ALU.subtract).then_inc(m_step.sem, 1)

            def add_root(b, n):
                _, _, w, pcs = pair(n)
                ww = w + len(pcs)
                z = Z[:, n % 2, :, 0:ww]
                dve.wait_ge(z_root.sem, z_root.at(b, n))
                dve.tensor_tensor(z, z, R[:, n % RB, :, 0:ww], ALU.add).then_inc(z_sum.sem, 1)

            def row_bias(b, n):
                _, hs, w, pcs = pair(n)
                k = hs[0] - HYP0
                dve.wait_ge(d_inv.sem, d_inv.at(b, n))
                dve.tensor_tensor(nb[:, n % 2, 0, :], R[:, n % RB, :, w], R[:, n % RB, :, w + len(pcs) - 1],
                                  ALU.max).then_inc(b_max.sem, 1)
                dve.wait_ge(b_max.sem, b_max.at(b, n))
                dve.tensor_tensor(nb[:, n % 2, 1, :], nb[:, n % 2, 0, :], root[:, 2, k:k + 2], ALU.mult) \
                    .then_inc(b_ready.sem, 1)

            def copy_turned(b, n, q):
                e, p = divmod(n, 2)
                i, x = ORDER[e], wide["turn", n, q]
                bank = wB[x % WB]
                if p == 0 and q == 0:
                    dve.wait_ge(h_valued.sem, h_valued.at(b, e - 1) if e else h_valued.before(b, NT - 1))
                dve.wait_ge(wide_full.sem, wide_full.at(b, x))
                js = [j for j, k in turns[n][q] if k == 0]
                below = [j for j in js if j < i]
                if below:
                    nb_ = len(below)
                    ins = dve.tensor_copy(PTh[:, below[0]:below[0] + nb_, 2 * p:2 * p + 2, :],
                                          bank[:, 0:nb_ * 2 * P].rearrange("p (j k t) -> p j k t", j=nb_, k=2))
                    if js[-1] != i:
                        ins.then_inc(wide_free.sem, 1)
                if js[-1] == i:
                    o = 2 * P * len(below)
                    dve.tensor_tensor(PTh[:, i, 2 * p:2 * p + 2, :],
                                      bank[:, o:o + 2 * P].rearrange("p (k t) -> p k t", k=2),
                                      masks[:, 0:1, :].to_broadcast([P, 2, P]), ALU.mult).then_inc(wide_free.sem, 1)

            def copy_hyp_sums(b, e):
                dve.wait_ge(h_valued.sem, h_valued.at(b, e))
                i, o = ORDER[e], P * (e % 4)
                dve.tensor_copy(O[:, 3, P * i:P * i + P], oH[:, o:o + P]).then_inc(h_copied.sem, 1)

            def copy_sums(b, m):
                g, c = divmod(m, 2)
                dve.wait_ge(valued.sem, valued.at(b, 12 * g + (3 if c == 0 else 11)))
                dve.tensor_copy(O[:, g, HB * c:HB * c + HB], oB[:]).then_inc(o_copied.sem, 1)

            def divide_sums(b, d, n, x):
                sums = wB[x % WB][:].rearrange("p (h w) -> p h w", w=VW)
                dve.wait_ge(wide_full.sem, wide_full.at(b, x))
                dve.reciprocal(rden[:, n % 2, :], sums[:, :, HD]).then_inc(y_inv.sem, 1)
                dve.wait_ge(y_inv.sem, y_inv.at(d, n))
                dve.tensor_tensor(Y[:, n], sums[:, :, 0:HD],
                                  rden[:, n % 2, :].unsqueeze(2).to_broadcast([P, H, HD]), ALU.mult) \
                    .then_inc(wide_free.sem, 1)

            def copy_rows(b, d, n, x):
                dve.wait_ge(wide_full.sem, wide_full.at(b, x))
                dve.tensor_copy(YT[:, n % 2].rearrange("p c t -> p (c t)"), wB[x % WB][:, 0:C]).then_inc(wide_free.sem, 1)

            def residual(b, d, n, x):
                if n == 0:
                    dve.wait_ge(x_here.sem, x_here.at(d))
                dve.wait_ge(wide_full.sem, wide_full.at(b, x))
                dve.tensor_tensor(X[:, n, :], X[:, n, :], wB[x % WB][:, 0:C], ALU.add).then_inc(wide_free.sem, 1)

            def late(b, d, item, index):
                x = index.get(item)
                kind = item[0]
                if kind == "turn_sums":
                    divide_sums(b, d, item[1], x)
                elif kind == "turn_rows":
                    copy_rows(b, d, item[1], x)
                elif kind == "project":
                    residual(b, d, item[1], x)
                elif kind == "statistics":
                    _, a, n0, n1 = item
                    if a == 0:
                        dve.wait_ge(wide_free.sem, wide_free.at(b, index["project", n1 - 1]))
                    else:
                        dve.wait_ge(biased.sem, biased.at(d))
                    for n in range(n0, n1):
                        dve.bn_stats(st[:, n, :], (X3 if a else X)[:, n, :]).then_inc(stats.sem, 1)
                elif kind == "variance":
                    a = item[1]
                    hold(dve, stats.sem, stats.at(d, 2 * NT * a + NT - 1), dve_passed)
                    for n in range(NT):
                        dve.bn_aggr(mv[:, n, :], st[:, n, :]).then_inc(stats.sem, 1)
                    dve.wait_ge(stats.sem, stats.at(d, 2 * NT * (a + 1) - 1))
                    dve.tensor_scalar(rs[:, 0], mv[:, :, 1], 1e-5, None, ALU.add).then_inc(var_ready.sem, 1)
                elif kind == "normalize":
                    a = item[1]
                    rows = X3 if a else X
                    dve.wait_ge(rs_exp.sem, rs_exp.at(d, a))

                    def step(k, ins):
                        ins.then_inc(rs_step.sem, 1)
                        dve.wait_ge(rs_step.sem, rs_step.at(d, 4 * a + k))

                    step(0, dve.tensor_tensor(rs[:, 2], rs[:, 0], rs[:, 1], ALU.mult))
                    step(1, dve.tensor_tensor(rs[:, 2], rs[:, 2], rs[:, 1], ALU.mult))
                    step(2, dve.tensor_scalar(rs[:, 2], rs[:, 2], -0.5, 1.5, ALU.mult, ALU.add))
                    step(3, dve.tensor_tensor(rs[:, 1], rs[:, 1], rs[:, 2], ALU.mult))
                    for n in range(NT):
                        ins = dve.tensor_scalar(rows[:, n, :], rows[:, n, :], mv[:, n, 0:1], rs[:, 1, n:n + 1],
                                                ALU.subtract, ALU.mult)
                    ins.then_inc(normed.sem, 1)
                elif kind == "add_bias":
                    dve.wait_ge(normed.sem, normed.at(d, 0))
                    dve.tensor_tensor(X3[:], X[:], bias2[:].unsqueeze(1).to_broadcast([P, NT, C]), ALU.add) \
                        .then_inc(biased.sem, 1)

            def out_free(b):
                dve.wait_ge(x3_sent.sem, x3_sent.before(b - 1))

            def do(b, item):
                kind = item[0]
                if kind == "argument":
                    clamp(b, *item[1:])
                elif kind == "maximum":
                    row_maximum(b, *item[1:])
                elif kind == "join_maxima":
                    join_maxima(b, item[1])
                elif kind == "turn_maxima":
                    cut_maxima(b, item[1])
                elif kind == "add_root":
                    add_root(b, item[1])
                elif kind == "row_bias":
                    row_bias(b, item[1])
                elif kind == "turn":
                    copy_turned(b, item[1], item[2])
                elif kind == "hyp_sums":
                    copy_hyp_sums(b, item[1])
                elif kind == "sums":
                    copy_sums(b, item[1])
                elif kind == "turn_sums":
                    divide_sums(b, b, item[1], wide[item])

            def turn(b, first=False):
                for step in work:
                    for slot in step:
                        for item in slot:
                            if not is_late(item):
                                do(b, item)
                            elif not first:
                                if item[0] == "add_bias":
                                    out_free(b)
                                late(b, b - 1, item, wide)
                            elif item[0] in RINGED:
                                dve.wait_ge(wide_full.sem, wide_full.at(b, wide[item]))
                                dve.wait_ge(wide_free.sem, wide_free.at(b, wide[item] - 1))
                                dve.sem_inc(wide_free.sem, 1)

            turn(0, first=True)
            with dve.Fori(1, B) as b:
                turn(b)
            for item in tail:
                if item[0] == "add_bias":
                    out_free(B)
                if item[0] != "inverse_root":
                    late(B, B - 1, item, tail_wide)


def experts(nc, io, x_mid):
    with ExitStack() as ctx:
        def sb(name, shape, dt=F32):
            return ctx.enter_context(nc.sbuf_tensor(name, shape, dt))

        def ev(name, per=1, step=1, carried=False):
            return Event(ctx, nc, name, per, step, carried)

        def sem(name):
            return ctx.enter_context(nc.semaphore(name))

        NF = FF // P
        UN = 4
        NK = HB // P
        ident = sb("e_ident", [P, P])
        bias = sb("e_bias", [P, C])
        idx = sb("e_index", [P, NT, TOPK], I32)
        idxf = sb("e_idxf", [P, NT, TOPK])
        ew = sb("e_ew", [P, NT, TOPK])
        picked = sb("e_picked", [P, NE, NT, TOPK])
        gate = sb("e_gate", [P, NE, NT])
        x = sb("e_x", [P, NT, C])
        acc = sb("e_acc", [P, NT, C])
        xT = sb("e_xT", [P, CK, N_TOK])
        w1 = sb("e_w1", [P, 2, CK, FF])
        w2 = sb("e_w2", [P, 2, NF, C])
        hT = sb("e_hT", [P, 2, NF, HB])
        st = sb("e_st", [P, NT, 6])
        mv = sb("e_mv", [P, NT, 2])
        rs = sb("e_rs", [P, 3, NT])
        hid = [ctx.enter_context(nc.psum_tensor(f"e_h{i}", [P, HB], F32)) for i in range(4)]
        yp = [ctx.enter_context(nc.psum_tensor(f"e_y{i}", [P, HB], F32)) for i in range(4)]
        consts = sem("e_consts")
        gates, turned, xt_ready, acc_ready = sem("e_gates"), sem("e_turned"), sem("e_xt_ready"), sem("e_acc_ready")
        w1_here = [ev(f"e_w1_here{i}", 1, 16) for i in range(2)]
        w2_here = [ev(f"e_w2_here{i}", 1, 16) for i in range(2)]
        hidden = ev("e_hidden", UN * NF, carried=True)
        gelu = ev("e_gelu", UN * NF, carried=True)
        mixed = ev("e_mixed", UN * NK, carried=True)
        added = ev("e_added", UN * NK, carried=True)
        st_done, ln_chain, normed = sem("e_st_done"), sem("e_ln_chain"), sem("e_normed")
        var_ready, root_ready, out_sent = sem("e_var"), sem("e_root"), sem("e_out_sent")
        TURNS = NE // 2
        block = ctx.enter_context(nc.Block())

        @block.sync
        def _(sp):
            sp.dma_start(x[:], x_mid[0].rearrange("(n p) c -> p n c", p=P)).then_inc(consts, 16)
            for dst, name in ((ident, "ident"), (bias, "ffn_b"), (idx, "e_idx"), (ew, "e_w")):
                sp.dma_start(dst[:], io[name]).then_inc(consts, 16)
            with sp.Fori(0, TURNS) as b:
                for i in range(2):
                    sp.wait_ge(hidden.sem, hidden.before(b, (2 * i + 2) * NF - 1))
                    sp.dma_start(w1[:, i], io["w1"][bass.ds(b * 2 + i, 1)].rearrange("o (c p) f -> p (o c) f", p=P)) \
                        .then_inc(w1_here[i].sem, 16)
                    sp.wait_ge(mixed.sem, mixed.before(b, (2 * i + 2) * NK - 1))
                    sp.dma_start(w2[:, i], io["w2"][bass.ds(b * 2 + i, 1)].rearrange("o (f p) c -> p (o f) c", p=P)) \
                        .then_inc(w2_here[i].sem, 16)
            sp.wait_ge(normed, 1)
            sp.dma_start(io["out"][0].rearrange("(n p) c -> p n c", p=P), acc[:]).then_inc(out_sent, 16)
            sp.wait_ge(out_sent, 16)

        @block.tensor
        def _(pe):
            hidden.start(pe)
            mixed.start(pe)
            pe.wait_ge(consts, 16 * 5)
            for c in range(CK):
                for half in range(2):
                    bank = hid[2 * c + half]
                    for n in range(4):
                        m = pe.transpose(bank[:, n * P:(n + 1) * P], x[:, 4 * half + n, c * P:(c + 1) * P], ident[:])
                    m.then_inc(turned, 1)
            pe.wait_ge(xt_ready, 4)
            with pe.Fori(0, TURNS) as b:
                def first(u):
                    i, c = divmod(u, 2)
                    if c == 0:
                        pe.wait_ge(w1_here[i].sem, w1_here[i].at(b))
                    for f in range(NF):
                        y = u * NF + f
                        pe.wait_ge(gelu.sem, gelu.at(b, y - 4) if y >= 4 else gelu.before(b, UN * NF - 4 + y))
                        for k in range(CK):
                            m = pe.matmul(hid[y % 4][:], w1[:, i, k, f * P:(f + 1) * P], xT[:, k, HB * c:HB * c + HB],
                                          start=(k == 0), stop=(k == CK - 1))
                        m.then_inc(hidden.sem, 1)

                def second(u):
                    i, c = divmod(u, 2)
                    if c == 0:
                        pe.wait_ge(w2_here[i].sem, w2_here[i].at(b))
                    pe.wait_ge(gelu.sem, gelu.at(b, (u + 1) * NF - 1))
                    for n in range(NK):
                        y = u * NK + n
                        pe.wait_ge(added.sem, added.at(b, y - 4) if y >= 4 else added.before(b, UN * NK - 4 + y))
                        for f in range(NF):
                            m = pe.matmul(yp[y % 4][:, 0:C], hT[:, u % 2, f, n * P:(n + 1) * P], w2[:, i, f, :],
                                          start=(f == 0), stop=(f == NF - 1))
                        m.then_inc(mixed.sem, 1)

                for u in range(UN + 1):
                    if u < UN:
                        first(u)
                    if u:
                        second(u - 1)

        @block.scalar
        def _(act):
            gelu.start(act)
            for c in range(CK):
                for half in range(2):
                    act.wait_ge(turned, 2 * c + half + 1)
                    act.activation(xT[:, c, HB * half:HB * half + HB], hid[2 * c + half][:], ACT.Copy).then_inc(xt_ready, 1)
            with act.Fori(0, TURNS) as b:
                for u in range(UN):
                    act.wait_ge(mixed.sem, mixed.at(b, (u - 1) * NK - 1) if u >= 2 else
                                mixed.before(b, (UN + u - 1) * NK - 1))
                    for f in range(NF):
                        y = u * NF + f
                        act.wait_ge(hidden.sem, hidden.at(b, y))
                        act.activation(hT[:, u % 2, f, :], hid[y % 4][:], ACT.Gelu).then_inc(gelu.sem, 1)
            act.preload_act_table_set("natural_log_exp_and_others")
            act.wait_ge(var_ready, 1)
            act.activation(rs[:, 1], rs[:, 0], ACT.Ln).then_inc(root_ready, 1)
            act.wait_ge(root_ready, 1)
            act.activation(rs[:, 1], rs[:, 1], ACT.Exp, scale=-0.5).then_inc(root_ready, 1)

        @block.vector
        def _(dve):
            added.start(dve)
            dve.wait_ge(consts, 16 * 5)
            dve.tensor_copy(idxf[:], idx[:]).then_inc(gates, 1)
            dve.wait_ge(gates, 1)
            for e in range(NE):
                dve.scalar_tensor_tensor(picked[:, e], idxf[:], float(e), ew[:], ALU.is_equal, ALU.mult).then_inc(gates, 1)
            dve.wait_ge(gates, 1 + NE)
            dve.tensor_tensor(gate[:], picked[:, :, :, 0], picked[:, :, :, 1], ALU.add).then_inc(gates, 1)
            dve.tensor_tensor(acc[:], x[:], bias[:].unsqueeze(1).to_broadcast([P, NT, C]), ALU.add).then_inc(acc_ready, 1)
            dve.wait_ge(acc_ready, 1)
            dve.wait_ge(gates, 2 + NE)
            with dve.Fori(0, TURNS) as b:
                for u in range(UN):
                    i, c = divmod(u, 2)
                    for n in range(NK):
                        y, tile = u * NK + n, NK * c + n
                        dve.wait_ge(mixed.sem, mixed.at(b, y))
                        dve.wait_ge(added.sem, added.at(b, y - 2 * NK) if y >= 2 * NK else
                                    added.before(b, (UN - 2) * NK + y))
                        dve.scalar_tensor_tensor(acc[:, tile, :], yp[y % 4][:, 0:C],
                                                 gate[:, bass.ds(b * 2 + i, 1), tile], acc[:, tile, :],
                                                 ALU.mult, ALU.add).then_inc(added.sem, 1)
            dve.wait_ge(added.sem, added.at(TURNS - 1, UN * NK - 1))
            for n in range(NT):
                dve.bn_stats(st[:, n, :], acc[:, n, :]).then_inc(st_done, 1)
            for n in range(NT):
                dve.wait_ge(st_done, n + 1)
                dve.bn_aggr(mv[:, n, :], st[:, n, :]).then_inc(st_done, 1)
            dve.wait_ge(st_done, 2 * NT)
            dve.tensor_scalar(rs[:, 0], mv[:, :, 1], 1e-5, None, ALU.add).then_inc(var_ready, 1)
            dve.wait_ge(root_ready, 2)

            def step(k, ins):
                ins.then_inc(ln_chain, 1)
                dve.wait_ge(ln_chain, k)

            step(1, dve.tensor_tensor(rs[:, 2], rs[:, 0], rs[:, 1], ALU.mult))
            step(2, dve.tensor_tensor(rs[:, 2], rs[:, 2], rs[:, 1], ALU.mult))
            step(3, dve.tensor_scalar(rs[:, 2], rs[:, 2], -0.5, 1.5, ALU.mult, ALU.add))
            step(4, dve.tensor_tensor(rs[:, 1], rs[:, 1], rs[:, 2], ALU.mult))
            for n in range(NT):
                ins = dve.tensor_scalar(acc[:, n, :], acc[:, n, :], mv[:, n, 0:1], rs[:, 1, n:n + 1],
                                        ALU.subtract, ALU.mult)
            ins.then_inc(normed, 1)


def shape_constants():
    d = np.arange(P) % HD
    pos = np.arange(T, dtype=np.float32)
    inv = (np.float32(1.0) / np.float32(10000.0) ** (np.arange(0, HD, 2, dtype=np.float32) / np.float32(HD))).astype(np.float32)
    ang = (pos[None, :] * inv[d % (HD // 2)][:, None]).astype(np.float32)
    tabs = np.stack([np.cos(ang), np.where(d < HD // 2, 1.0, -1.0)[:, None] * np.sin(ang)], 1).astype(np.float32)
    rowind = np.zeros((P, 4, 16), np.float32)
    for g, first in enumerate((GW, 0, 0, GW)):
        for j in range(GW):
            h = first + j
            row = None
            if HYP0 <= h < COS0:
                row = h - HYP0 + (N_HYP if g >= 2 else 0)
            elif h >= COS0 and g >= 2:
                row = 2 * N_HYP + h - COS0
            if row is not None:
                rowind[j * HD:(j + 1) * HD, g, row] = 1.0
    cos_rows = (np.arange(P) // HD + GW) >= COS0
    blk = (np.arange(P)[:, None] // HD == np.arange(P)[None, :] // HD) & cos_rows[None, :]
    v_pad = np.zeros((P, 4, NT, 4, VW), np.float32)
    v_pad[..., HD] = 1.0
    first, second = np.arange(P)[:, None], np.arange(P)[None, :]
    masks = np.stack([second >= first, np.where(second < first, -1e25, 0.0), np.where(second > first, -1e25, 0.0),
                      np.where(second > first, 1e9, 0.0)], 1).astype(np.float32)
    return {
        "masks": masks,
        "ident": np.eye(P, dtype=np.float32),
        "tabs": tabs,
        "rowind": rowind,
        "blk": blk.astype(np.float32),
        "nhyp": (~cos_rows).astype(np.float32)[:, None],
        "v_pad": v_pad,
    }


def lay_out(L0_attn_x, L0_attn_qkv_w, L0_attn_curvature, L0_attn_proj_w, L0_attn_proj_b, L0_ffn_bias,
            L0_ffn_w1, L0_ffn_w2, L0_ffn_expert_indices, L0_ffn_expert_weights, L0_ffn_scores):
    w = np.asarray(L0_attn_qkv_w)
    swap = np.arange(2 * C).reshape(-1, 2, HD // 2)[:, ::-1].reshape(-1)
    packed = np.concatenate([np.arange(h * HD, h * HD + HD) for h in PACKED])
    w_all = np.concatenate([w[:2 * C], w[:2 * C][swap], w[2 * C:][packed]], 0)
    curv = np.asarray(L0_attn_curvature).reshape(-1)
    kcurv = np.zeros((P, 2, 2), np.float32)
    rcurv = np.zeros((16, 3), np.float32)
    rcurv[:, 0] = 1.0
    rcurv[0:N_HYP, 1] = 1.0
    rcurv[N_HYP:2 * N_HYP, 2] = 1.0
    kcurv[:, :, 1] = 1.0
    for i in range(N_HYP):
        g, row = (HYP0 + i) // GW, (HYP0 + i) % GW * HD
        kcurv[row:row + HD, g, 0] = curv[i]
        kcurv[row:row + HD, g, 1] = 0.0
        rcurv[[i, N_HYP + i], 0] = curv[i]
    return {
        "x": np.ascontiguousarray(L0_attn_x),
        "w_qkv": np.ascontiguousarray(w_all.T.reshape(CK, P, -1).transpose(1, 0, 2)),
        "acurv": np.ascontiguousarray(np.broadcast_to(curv, (P, N_HYP))),
        "w_proj": np.ascontiguousarray(np.asarray(L0_attn_proj_w).T[packed].reshape(CK, P, C).transpose(1, 0, 2)),
        "proj_b": np.asarray(L0_attn_proj_b)[None, :],
        "ffn_b": np.ascontiguousarray(np.broadcast_to(np.asarray(L0_ffn_bias), (P, C))),
        "w1": np.ascontiguousarray(L0_ffn_w1),
        "w2": np.ascontiguousarray(L0_ffn_w2),
        "e_idx": np.ascontiguousarray(np.asarray(L0_ffn_expert_indices).reshape(NT, P, TOPK).transpose(1, 0, 2)),
        "e_w": np.ascontiguousarray(np.asarray(L0_ffn_expert_weights).reshape(NT, P, TOPK).transpose(1, 0, 2)),
        "kcurv": kcurv,
        "rcurv": rcurv,
    }


def build(nc, io):
    def scratch(name, shape, dt=F32):
        return nc.dram_tensor(name, shape, dt, kind="Internal").ap()

    qk_parts = scratch("qk_parts", [B, 2, 3, C, T], BF16)
    t_parts = scratch("t_parts", [B, 2 * N_HYP, 3, T], BF16)
    v_rows = scratch("v_rows", [B, P, 4 * NT * 4 * VW])
    rk_cols = scratch("rk_cols", [B, P, NT * N_COS])
    m_parts = scratch("m_parts", [N_DOT * NT, 3, P], BF16)
    x_mid = scratch("x_mid", [B, T, C])
    project(nc, io, qk_parts, t_parts, v_rows, rk_cols)
    attend(nc, io, qk_parts, t_parts, v_rows, rk_cols, m_parts, x_mid)
    experts(nc, io, x_mid)


def kernel(**inputs):
    import concourse.bacc as bacc
    from concourse.bass_utils import run_bass_kernel_spmd

    nc = bacc.Bacc("TRN2", target_bir_lowering=False, num_devices=1)
    arrays = {f"in_{n}": np.asarray(a) for n, a in {**shape_constants(), **lay_out(**inputs)}.items()}
    io = {n[3:]: nc.dram_tensor(n, a.shape, mybir.dt.from_np(a.dtype), kind="ExternalInput").ap()
          for n, a in arrays.items()}
    io["out"] = nc.dram_tensor("out", (B, T, C), F32, kind="ExternalOutput").ap()
    build(nc, io)
    return run_bass_kernel_spmd(nc, [arrays], core_ids=[0]).results[0]["out"]
```
